# Optimizing a Trainium2 kernel written in Bass

```python
import numpy as np
import jax
import jax.numpy as jnp

def _softmax(x, axis=-1):
    return jax.nn.softmax(x, axis=axis)
def _gelu(x):
    return jax.nn.gelu(x, approximate=True)
def _silu(x):
    return jax.nn.silu(x)
def _sigmoid(x):
    return jax.nn.sigmoid(x)
def _layernorm(x, axis=-1, eps=1e-5):
    m = jnp.mean(x, axis=axis, keepdims=True)
    v = jnp.var(x, axis=axis, keepdims=True)
    return (x - m) / jnp.sqrt(v + eps)
def _scatter_add(tgt, idx, src, axis=0):
    return tgt.at[idx].add(src)
def _segment_sum(src, seg, n):
    return jax.ops.segment_sum(src, seg, n)

kernel_name = 'mk_conv_seq_d1_conv_nchw512_743dbc'

def setup_inputs(seed: int = 0):
    np.random.seed(seed)
    _w = jnp.asarray
    def _rec_inputs():
        import jax
        import jax.numpy as jnp
        _gk = jax.random.key(seed)
        x = 7.22e-05 + 1 * jax.random.normal(jax.random.fold_in(_gk, 1), (4, 512, 64, 64), jnp.float32)
        return x
    x = _rec_inputs()
    def _L0_conv_setup():
        import jax, jax.numpy as jnp
        import numpy as np
        B, C, H, W = (4, 512, 64, 64)
        NH, R = (8, 2)
        DK = C // NH
        EPS = 1e-05

        def _conv(x, w, stride):
            return jax.lax.conv_general_dilated(x, w, window_strides=(stride, stride), padding='VALID', dimension_numbers=('NCHW', 'OIHW', 'NCHW'))
        key = jax.random.key(seed)
        ks = jax.random.split(key, 5)
        x = jax.random.normal(ks[0], (B, C, H, W), dtype=jnp.float32)
        Wq = jax.random.normal(ks[1], (C, C, 1, 1), dtype=jnp.float32) * 0.02
        Wk = jax.random.normal(ks[2], (C, C, R, R), dtype=jnp.float32) * 0.02
        Wv = jax.random.normal(ks[3], (C, C, R, R), dtype=jnp.float32) * 0.02
        Wproj = jax.random.normal(ks[4], (C, C, 1, 1), dtype=jnp.float32) * 0.02
        bias = jnp.zeros((1, NH, 1, 1), dtype=jnp.float32)
        bn_gamma = jnp.ones((C,), dtype=jnp.float32)
        bn_beta = jnp.zeros((C,), dtype=jnp.float32)
        ln_gamma = jnp.ones((C,), dtype=jnp.float32)
        ln_beta = jnp.zeros((C,), dtype=jnp.float32)
        return {'x': x, 'Wq': Wq, 'Wk': Wk, 'Wv': Wv, 'bias': bias, 'Wproj': Wproj, 'bn_gamma': bn_gamma, 'bn_beta': bn_beta, 'ln_gamma': ln_gamma, 'ln_beta': ln_beta}
    _L0_conv_all = _L0_conv_setup()
    _L0_conv_in = {k: v for k, v in _L0_conv_all.items() if k in ('Wq', 'Wk', 'Wv', 'bias', 'Wproj', 'bn_gamma', 'bn_beta', 'ln_gamma', 'ln_beta', )}
    del _L0_conv_all

    return {
        "x": x,
        "L0_conv_Wq": _L0_conv_in["Wq"],
        "L0_conv_Wk": _L0_conv_in["Wk"],
        "L0_conv_Wv": _L0_conv_in["Wv"],
        "L0_conv_bias": _L0_conv_in["bias"],
        "L0_conv_Wproj": _L0_conv_in["Wproj"],
        "L0_conv_bn_gamma": _L0_conv_in["bn_gamma"],
        "L0_conv_bn_beta": _L0_conv_in["bn_beta"],
        "L0_conv_ln_gamma": _L0_conv_in["ln_gamma"],
        "L0_conv_ln_beta": _L0_conv_in["ln_beta"],
    }

def reference(x, L0_conv_Wq, L0_conv_Wk, L0_conv_Wv, L0_conv_bias, L0_conv_Wproj, L0_conv_bn_gamma, L0_conv_bn_beta, L0_conv_ln_gamma, L0_conv_ln_beta):
    import jax
    import jax.numpy as jnp
    def _L0_conv_ref(x, Wq, Wk, Wv, bias, Wproj, bn_gamma, bn_beta, ln_gamma, ln_beta):
        import jax, jax.numpy as jnp
        import numpy as np
        B, C, H, W = (4, 512, 64, 64)
        NH, R = (8, 2)
        DK = C // NH
        EPS = 1e-05

        def _conv(x, w, stride):
            return jax.lax.conv_general_dilated(x, w, window_strides=(stride, stride), padding='VALID', dimension_numbers=('NCHW', 'OIHW', 'NCHW'))
        b, c, h, w = x.shape
        r = Wk.shape[2]
        n = h * w
        scale = DK ** (-0.5)
        Q = _conv(x, Wq, 1)
        K = _conv(x, Wk, r)
        V = _conv(x, Wv, r)
        hr, wr = (K.shape[2], K.shape[3])
        nr = hr * wr
        Qh = Q.reshape(b, NH, DK, n).transpose(0, 1, 3, 2)
        Kh = K.reshape(b, NH, DK, nr).transpose(0, 1, 3, 2)
        Vh = V.reshape(b, NH, DK, nr).transpose(0, 1, 3, 2)
        attn = jnp.einsum('bhnd,bhmd->bhnm', Qh, Kh) * scale + bias
        attn = jax.nn.softmax(attn, axis=-1)
        out = jnp.einsum('bhnm,bhmd->bhnd', attn, Vh)
        out = out.transpose(0, 1, 3, 2).reshape(b, c, h, w)
        p = _conv(out, Wproj, 1)
        mu = p.mean(axis=(0, 2, 3), keepdims=True)
        var = p.var(axis=(0, 2, 3), keepdims=True)
        p = (p - mu) * jax.lax.rsqrt(var + EPS)
        p = p * bn_gamma[None, :, None, None] + bn_beta[None, :, None, None]
        y = x + p
        yt = y.transpose(0, 2, 3, 1)
        mu2 = yt.mean(axis=-1, keepdims=True)
        var2 = yt.var(axis=-1, keepdims=True)
        yt = (yt - mu2) * jax.lax.rsqrt(var2 + EPS) * ln_gamma + ln_beta
        return yt.transpose(0, 3, 1, 2)

    def _gn(v, G=32, eps=1e-5):
        B_, C_, H_, W_ = v.shape
        g = v.reshape(B_, G, C_ // G, H_, W_)
        m = jnp.mean(g, axis=(2, 3, 4), keepdims=True)
        s = jnp.var(g, axis=(2, 3, 4), keepdims=True)
        return ((g - m) / jnp.sqrt(s + eps)).reshape(v.shape)

    def _ln_c(v, eps=1e-6):
        m = jnp.mean(v, axis=1, keepdims=True)
        s = jnp.var(v, axis=1, keepdims=True)
        return (v - m) / jnp.sqrt(s + eps)

    def _ln_t(v, eps=1e-5):
        m = jnp.mean(v, axis=-1, keepdims=True)
        s = jnp.var(v, axis=-1, keepdims=True)
        return (v - m) / jnp.sqrt(s + eps)

    def _to_tokens(v):
        B_, C_, H_, W_ = v.shape
        return v.reshape(B_, C_, H_ * W_).transpose(0, 2, 1)
    def _from_tokens(t, like):
        B_, C_, H_, W_ = like.shape
        return t.transpose(0, 2, 1).reshape(B_, C_, H_, W_)

    x = _L0_conv_ref(x, L0_conv_Wq, L0_conv_Wk, L0_conv_Wv, L0_conv_bias, L0_conv_Wproj, L0_conv_bn_gamma, L0_conv_bn_beta, L0_conv_ln_gamma, L0_conv_ln_beta)
    return x


_drawn_inputs = setup_inputs


def setup_inputs(seed=0):
    import zlib

    import numpy as np

    out = dict(_drawn_inputs(seed))
    spreads = {'L0_conv_bias': (0.0, 0.1),
     'L0_conv_bn_gamma': (1.0, 0.2),
     'L0_conv_bn_beta': (0.0, 0.1),
     'L0_conv_ln_gamma': (1.0, 0.2),
     'L0_conv_ln_beta': (0.0, 0.1)}
    factors = {}
    for name, (base, spread) in spreads.items():
        noise = np.random.default_rng([zlib.crc32(name.encode()), seed]).standard_normal(out[name].shape)
        drawn = base * np.exp(spread * noise) if base else spread * noise
        out[name] = jnp.asarray(drawn.astype(out[name].dtype))
    for name, factor in factors.items():
        out[name] = (out[name] * factor).astype(out[name].dtype)
    return out
```

```python
from contextlib import ExitStack

import concourse.bass as bass
from concourse import mybir

ALU = mybir.AluOpType
ACT = mybir.ActivationFunctionType
AX = mybir.AxisListType
F32 = mybir.dt.float32
F32R = mybir.dt.float32r
F16 = mybir.dt.float16

P = 128
NH = 8
R = 2
RS = R * R
EPS = 1e-5
P_SCALE = 4096.0
V_SCALE = 1024.0
TINY = 1e-30


def wait(eng, semaphore, value):
    if not isinstance(value, int) or value > 0:
        eng.wait_ge(semaphore, value)


def there(i, n):
    return not isinstance(i, int) or 0 <= i < n


def conv_attention(nc, x, wq, wk, wv, bias, wp, bn_gamma, bn_beta, ln_gamma, ln_beta, out):
    B, C, H, W = x.shape
    CT = C // P
    DK = C // NH
    NR = H * W // RS
    CH = 512
    NCH = H * W // CH
    MT = NR // P
    ROWS = CH // W
    assert NCH == MT and CH // RS == P and DK * 2 == P

    k_scr = nc.dram_tensor("k_scr", (B, NH, 2, DK, NR), F32, kind="Internal").ap()
    v_scr = nc.dram_tensor("v_scr", (B, 2, MT, P, C), F16, kind="Internal").ap()
    f_scr = nc.dram_tensor("f_scr", (B, P, CT), F32, kind="Internal").ap()
    p_scr = nc.dram_tensor("p_scr", (B * NCH, CT, P, CH), F32, kind="Internal").ap()

    x_chunks = x.rearrange("b (ct p) (t r) w -> b t p ct (r w)", p=P, r=ROWS)
    out_chunks = out.rearrange("b (ct p) (t r) w -> b t p ct (r w)", p=P, r=ROWS)

    with ExitStack() as whole:
        ident = whole.enter_context(nc.sbuf_tensor("ident", [P, P], F32))
        stats = whole.enter_context(nc.sbuf_tensor("stats", [P, CT, B * NCH, 6], F32))
        keys_and_values(nc, x_chunks, wk, wv, ident, k_scr, v_scr, f_scr, B, C, CT, MT, CH, W)
        attention(nc, x_chunks, wq, wp, bias, ident, stats, k_scr, v_scr, f_scr, p_scr,
                  B, C, CT, NR, MT, CH, NCH, DK)
        norms(nc, x_chunks, out_chunks, p_scr, stats, bn_gamma, bn_beta, ln_gamma, ln_beta,
              B, C, CT, CH, NCH)


def keys_and_values(nc, x_chunks, wk, wv, ident, k_scr, v_scr, f_scr, B, C, CT, MT, CH, W):
    KT = CT * RS
    VB = 4
    SLICES = 2 * KT
    with ExitStack() as ctx:
        def sb(name, shape, dt=F32):
            return ctx.enter_context(nc.sbuf_tensor(name, shape, dt))

        def psum(name):
            return ctx.enter_context(nc.psum_tensor(name, [P, CH], F32))

        def sem(name):
            return ctx.enter_context(nc.semaphore(name))

        w_hi = sb("w_hi", [P, SLICES, C], F32R)
        w_lo = sb("w_lo", [P, SLICES, C], F32R)
        x_in = sb("x1_in", [P, CT, CH])
        x_hi = sb("x1_hi", [P, 2, CT, RS, P], F32R)
        x_lo = sb("x1_lo", [P, 2, CT, RS, P], F32R)
        v_all = sb("v_all", [P, MT, C])
        k_nat = sb("k_nat", [P, C])
        k_hi = sb("k_hi", [P, CT, P], F32R)
        k_lo = sb("k_lo", [P, CT, P], F32R)
        v_parts = sb("v_parts", [P, VB, 2, C], F16)
        v_abs = sb("v_abs", [P, C])
        v_row = sb("v_row", [P, C])
        v_max = sb("v_max", [P, CT])
        v_div = sb("v_div", [P, CT])
        v_inv = sb("v_inv", [P, CT])
        v_fac = sb("v_fac", [P, CT])
        ones = sb("ones1", [P, P])

        k_ps = [psum(f"k_ps{i}") for i in range(2)]
        v_ps = [psum(f"v_ps{i}") for i in range(2)]
        t_ps = psum("t_ps")
        m_ps = psum("m_ps")

        consts = sem("consts1")
        w_landed = [sem(f"w_landed{i}") for i in range(MT)]
        w_hi_done = sem("w_hi_done")
        w_lo_done = sem("w_lo_done")
        x0_landed = [sem(f"x0_landed{ct}") for ct in range(CT)]
        x_landed = sem("x1_landed")
        x_hi_done = sem("x1_hi_done")
        x_lo_done = sem("x1_lo_done")
        k_sum = sem("k_sum")
        v_sum = sem("v_sum")
        k_copied = sem("k_copied")
        v_copied = sem("v_copied")
        k_turned = sem("k_turned")
        k_hi_done = sem("k_hi_done")
        k_lo_done = sem("k_lo_done")
        k_stored = sem("k_stored")
        abs_done = sem("abs_done")
        abs_turned = sem("abs_turned")
        vmax_steps = sem("vmax_steps")
        vdiag_done = sem("vdiag_done")
        vrow_sum = sem("vrow_sum")
        vrow_done = sem("vrow_done")
        v_scaled = sem("v_scaled")
        v_hi_done = sem("v_hi_done")
        v_lo_done = sem("v_lo_done")
        v_stored = [sem(f"v_stored{i}") for i in range(VB)]
        f_stored = sem("f_stored")

        x_taps = x_in.rearrange("p ct (i r j s) -> p ct r s i j", r=R, s=R, j=W // R)
        k_dst = k_scr.rearrange("b (ct hh) s d (t m) -> b s hh t d ct m", hh=2, m=P)

        with nc.Block() as block:

            @block.sync
            def _(sp):
                for ct in range(CT):
                    sp.dma_start(x_in[:, ct, :], x_chunks[0, 0, :, ct]).then_inc(x0_landed[ct], 16)
                for i in range(SLICES):
                    kt = i % KT
                    if i >= MT:
                        sp.wait_ge(w_lo_done, i - MT + 1)
                    src = (wk, wv)[i // KT][(kt // RS) * P:(kt // RS + 1) * P, kt % RS, :]
                    sp.dma_start(v_all[:, i % MT, :], src).then_inc(w_landed[i % MT], 16)
                with sp.Fori(1, MT) as i:
                    sp.wait_ge(x_lo_done, i + 1)
                    sp.dma_start(x_in[:, :, :], x_chunks[0, i]).then_inc(x_landed, 16)
                with sp.Fori(1, B) as b:
                    with sp.Fori(0, MT) as i:
                        sp.wait_ge(x_lo_done, b * MT + i + 1)
                        sp.dma_start(x_in[:, :, :], x_chunks[b, i]).then_inc(x_landed, 16)

            @block.gpsimd
            def _(pool):
                nc.gpsimd.memset(ident[:, :], 0.0).then_inc(consts, 1)
                nc.gpsimd.memset(ones[:, :], 1.0).then_inc(consts, 1)
                pool.wait_ge(consts, 2)
                nc.gpsimd.affine_select(out=ident[:, :], in_=ident[:, :], compare_op=ALU.not_equal,
                                        fill=1.0, base=0, pattern=[[-1, P]],
                                        channel_multiplier=1).then_inc(consts, 1)
                pool.sem_inc(x_lo_done, 1)
                pool.sem_inc(x_landed, 16)
                for ct in range(CT):
                    pool.wait_ge(x0_landed[ct], 16)
                with pool.Fori(0, B * MT // 2) as u:
                    for j in range(2):
                        t = u * 2 + j
                        pool.wait_ge(x_landed, 16 * t + 16)
                        pool.wait_ge(v_sum, t + 1)
                        for ct in range(CT):
                            for r in range(R):
                                last = nc.gpsimd.tensor_tensor(
                                    x_hi[:, j, ct, 2 * r:2 * r + 2, :].rearrange("p s (i j) -> p s i j", j=W // R),
                                    x_taps[:, ct, r], ones[:, 0:P].rearrange("p (s i j) -> p s i j", s=1, j=W // R
                                                                             ).to_broadcast([P, R, P // (W // R), W // R]),
                                    ALU.mult)
                        last.then_inc(x_hi_done, 1)
                        pool.wait_ge(x_hi_done, t + 1)
                        for ct in range(CT):
                            for r in range(R):
                                out = x_lo[:, j, ct, 2 * r:2 * r + 2, :].rearrange("p s (i j) -> p s i j", j=W // R)
                                hi = x_hi[:, j, ct, 2 * r:2 * r + 2, :].rearrange("p s (i j) -> p s i j", j=W // R)
                                last = nc.gpsimd.tensor_tensor(out, x_taps[:, ct, r], hi, ALU.subtract)
                        last.then_inc(x_lo_done, 1)

            @block.tensor
            def _(pe):
                pe.sem_inc(v_sum, 2)
                pe.sem_inc(k_turned, 1)
                pe.sem_inc(vrow_sum, 1)
                pe.wait_ge(consts, 3)
                with pe.Fori(0, B) as b:
                    with pe.Fori(0, MT // 2) as u:
                        for j in range(2):
                            t = b * MT + u * 2 + j
                            pe.wait_ge(x_lo_done, t + 2)
                            for kv, (ps, copied, done) in enumerate(((k_ps, k_copied, k_sum),
                                                                     (v_ps, v_copied, v_sum))):
                                pe.wait_ge(copied, t + 1)
                                for kt in range(KT):
                                    if kt % 2 == 0:
                                        pe.wait_ge(w_lo_done, kv * KT + kt + 2)
                                    hi = x_hi[:, j, kt // RS, kt % RS, :]
                                    lo = x_lo[:, j, kt // RS, kt % RS, :]
                                    for n, (a, w) in enumerate(((hi, w_hi), (hi, w_lo), (lo, w_hi))):
                                        mm = nc.tensor.matmul(ps[j][:, :], a, w[:, kv * KT + kt, :],
                                                              start=(kt == 0 and n == 0),
                                                              stop=(kt == KT - 1 and n == 2))
                                mm.then_inc(done, 1)
                            pe.wait_ge(k_copied, t + 3)
                            pe.wait_ge(k_lo_done, t + 1)
                            for ct in range(CT):
                                mm = nc.tensor.transpose(t_ps[:, ct * P:(ct + 1) * P],
                                                         k_nat[:, ct * P:(ct + 1) * P], ident[:, :])
                            mm.then_inc(k_turned, 1)
                    pe.wait_ge(abs_done, b + 1)
                    pe.wait_ge(vrow_done, b + 1)
                    for ct in range(CT):
                        mm = nc.tensor.transpose(m_ps[:, ct * P:(ct + 1) * P],
                                                 v_abs[:, ct * P:(ct + 1) * P], ident[:, :])
                    mm.then_inc(abs_turned, 1)
                    pe.wait_ge(vdiag_done, b + 1)
                    nc.tensor.matmul(m_ps[:, :], ones[:, :], v_abs[:, :], start=True, stop=True
                                     ).then_inc(vrow_sum, 1)

            @block.scalar
            def _(act):
                act.sem_inc(k_copied, 2)
                act.sem_inc(v_copied, 2)
                act.sem_inc(vrow_done, 1)
                act.sem_inc(k_stored, 64)
                act.sem_inc(f_stored, 16)
                for s in range(VB):
                    act.sem_inc(v_stored[s], 16)
                for i in range(SLICES):
                    act.wait_ge(w_landed[i % MT], 16 * (i // MT + 1))
                    nc.scalar.copy(w_hi[:, i, :], v_all[:, i % MT, :]).then_inc(w_hi_done, 1)
                with act.Fori(0, B) as b:
                    with act.Fori(0, MT // 2) as u:
                        for j in range(2):
                            t = b * MT + u * 2 + j
                            act.wait_ge(k_sum, t + 1)
                            act.wait_ge(k_turned, t + 1)
                            nc.scalar.copy(k_nat[:, :], k_ps[j][:, :]).then_inc(k_copied, 1)
                            act.wait_ge(v_sum, t + 3)
                            act.wait_ge(v_lo_done, t + 1)
                            nc.scalar.copy(v_all[:, u * 2 + j, :], v_ps[j][:, :]).then_inc(v_copied, 1)
                            act.wait_ge(k_turned, t + 2)
                            act.wait_ge(k_stored, 64 * t + 64)
                            nc.scalar.copy(k_hi[:, :, :], t_ps.rearrange("p (ct m) -> p ct m", m=P)
                                           ).then_inc(k_hi_done, 1)
                            act.wait_ge(k_lo_done, t + 2)
                            for part, src in enumerate((k_hi, k_lo)):
                                for hh in range(2):
                                    act.dma_start(k_dst[b, part, hh, u * 2 + j],
                                                  src[hh * 64:(hh + 1) * 64, :, :].bitcast(F32)).then_inc(k_stored, 16)
                    act.wait_ge(vrow_sum, b + 2)
                    act.wait_ge(v_scaled, MT * b + MT)
                    nc.scalar.copy(v_row[:, :], m_ps[:, :]).then_inc(vrow_done, 1)
                    act.dma_start(f_scr[b], v_fac[:, :]).then_inc(f_stored, 16)
                    for i in range(MT + 1):
                        if i < MT:
                            act.wait_ge(v_scaled, MT * b + MT + i + 1)
                            act.wait_ge(v_stored[i % VB], 16 * (b * (MT // VB) + i // VB + 1))
                            nc.scalar.copy(v_parts[:, i % VB, 0], v_all[:, i, :]).then_inc(v_hi_done, 1)
                        if i:
                            act.wait_ge(v_lo_done, MT * b + MT + i)
                            act.dma_start(v_scr[b, :, i - 1].rearrange("s m c -> m s c"),
                                          v_parts[:, (i - 1) % VB]).then_inc(v_stored[(i - 1) % VB], 16)
                act.wait_ge(k_stored, 64 * (B * MT + 1))
                act.wait_ge(f_stored, 16 * (B + 1))
                for s in range(VB):
                    act.wait_ge(v_stored[s], 16 * (B * MT // VB + 1))

            def split_v(dve, b, i):
                dve.wait_ge(v_hi_done, MT * b + i + 1)
                nc.vector.tensor_tensor(v_parts[:, i % VB, 1], v_all[:, i, :], v_parts[:, i % VB, 0],
                                        ALU.subtract).then_inc(v_lo_done, 1)

            @block.vector
            def _(dve):
                dve.sem_inc(k_lo_done, 1)
                dve.sem_inc(v_scaled, MT)
                dve.sem_inc(v_lo_done, MT)
                for i in range(SLICES):
                    dve.wait_ge(w_hi_done, i + 1)
                    nc.vector.tensor_tensor(w_lo[:, i, :], v_all[:, i % MT, :], w_hi[:, i, :],
                                            ALU.subtract).then_inc(w_lo_done, 1)
                with dve.Fori(0, B) as b:
                    with dve.Fori(0, MT) as i:
                        t = b * MT + i
                        dve.wait_ge(k_hi_done, t + 1)
                        nc.vector.tensor_tensor(k_lo[:, :, :], t_ps.rearrange("p (ct m) -> p ct m", m=P),
                                                k_hi[:, :, :], ALU.subtract).then_inc(k_lo_done, 1)
                    dve.wait_ge(v_copied, MT * b + MT + 2)
                    dve.wait_ge(vrow_sum, b + 1)
                    nc.vector.tensor_reduce(v_abs[:, :], v_all.rearrange("p t c -> p c t"), AX.X, ALU.max,
                                            apply_absolute_value=True).then_inc(abs_done, 1)
                    dve.wait_ge(abs_turned, b + 1)
                    nc.vector.tensor_reduce(v_max[:, :], m_ps.rearrange("p (ct m) -> p ct m", m=P),
                                            AX.X, ALU.max).then_inc(vmax_steps, 1)
                    dve.wait_ge(vmax_steps, 4 * b + 1)
                    nc.vector.tensor_scalar(v_div[:, :], v_max[:, :], TINY, 1.0 / V_SCALE, ALU.max,
                                            ALU.mult).then_inc(vmax_steps, 1)
                    dve.wait_ge(vmax_steps, 4 * b + 2)
                    nc.vector.reciprocal(v_inv[:, :], v_div[:, :]).then_inc(vmax_steps, 1)
                    dve.wait_ge(f_stored, 16 * b + 16)
                    nc.vector.tensor_scalar(v_fac[:, :], v_div[:, :], 1.0 / P_SCALE, None,
                                            ALU.mult).then_inc(vmax_steps, 1)
                    dve.wait_ge(vmax_steps, 4 * b + 4)
                    for ct in range(CT):
                        last = nc.vector.tensor_scalar(v_abs[:, ct * P:(ct + 1) * P], ident[:, :],
                                                       v_inv[:, ct:ct + 1], None, ALU.mult)
                    last.then_inc(vdiag_done, 1)
                    dve.wait_ge(vrow_done, b + 2)
                    for i in range(MT):
                        nc.vector.tensor_tensor(v_all[:, i, :], v_all[:, i, :], v_row[:, :], ALU.mult
                                                ).then_inc(v_scaled, 1)
                        if i:
                            split_v(dve, b, i - 1)
                    split_v(dve, b, MT - 1)


def attention(nc, x_chunks, wq, wp, bias, ident, stats, k_scr, v_scr, f_scr, p_scr,
              B, C, CT, NR, MT, CH, NCH, DK):
    CHUNKS = B * NCH
    CU, CG, CP = 4 * NH, NH, CT
    UNITS, GROUPS, PAIRS, TILES = CHUNKS * CU, CHUNKS * CG, CHUNKS * CP, CHUNKS * CT
    HALF = CH // 2
    SCALE = float(DK) ** -0.5
    assert SCALE == 0.125
    with ExitStack() as ctx:
        def sb(name, shape, dt=F32):
            return ctx.enter_context(nc.sbuf_tensor(name, shape, dt))

        def psum(name, n=1):
            return ctx.enter_context(nc.psum_tensor(name, [P, n * CH], F32))

        def sem(name):
            return ctx.enter_context(nc.semaphore(name))

        k_sb = sb("k_sb", [P, NH, NR], F32R)
        vh_sb = sb("vh_sb", [P, MT, C], F16)
        vl_sb = sb("vl_sb", [P, MT, C], F16)
        f_sb = sb("f_sb", [P, CP, CT])
        wq_hi = sb("wq_hi", [P, CT, C], F32R)
        wq_lo = sb("wq_lo", [P, CT, C], F32R)
        wp_hi = sb("wp_hi", [P, CT, C], F32R)
        wp_lo = sb("wp_lo", [P, CT, C], F32R)
        x_in = sb("x2_in", [P, CT, CH])
        x_hi = sb("x2_hi", [P, CT, CH], F32R)
        x_lo = sb("x2_lo", [P, CT, CH], F32R)
        q_x = sb("q_x", [P, 2, 2, CH], F32R)
        q_y = sb("q_y", [P, 2, 2, CH], F32R)
        probs = sb("probs", [P, 2, NR])
        pt_hi = sb("pt_hi", [P, 2, 2, MT, HALF], F16)
        pt_lo = sb("pt_lo", [P, 2, 2, MT, HALF], F16)
        neg_max = sb("neg_max", [P, 2])
        shift = sb("shift", [P, 2])
        ones = sb("ones2", [P, P])
        bias_sb = sb("bias_sb", [P, NH])
        sums = sb("sums", [P, 2, 2, 2])
        inv = sb("inv", [P, 2, 2])
        inv_wide = sb("inv_wide", [P, 2, 2, DK])
        spread = sb("spread", [P, HALF])
        o_sb = sb("o_sb", [P, 2, HALF])
        o_hi = sb("o_hi", [P, 2, CT, CH], F32R)
        o_lo = sb("o_lo", [P, 2, CT, CH], F32R)
        proj = sb("proj", [P, 2, CH])

        s_ps = [psum(f"s_ps{i}", 2) for i in range(2)]
        t_ps = [psum(f"t2_ps{i}") for i in range(2)]
        pv_ps = psum("pv_ps")
        g_ps = psum("g_ps")

        w_landed = [sem(f"w2_landed{i}") for i in range(2 * CT)]
        w_hi_done = sem("w2_hi_done")
        w_lo_done = sem("w2_lo_done")
        bias_landed = sem("bias_landed")
        x0_landed = sem("x20_landed")
        x_landed = sem("x2_landed")
        x_hi_done = sem("x2_hi_done")
        x_lo_done = sem("x2_lo_done")
        k_landed = [sem(f"k_landed{p}") for p in range(CP)]
        v_landed = [sem(f"v_landed{p}") for p in range(CP)]
        q_sum = sem("q_sum")
        q_hi_done = sem("q_hi_done")
        q_lo_done = sem("q_lo_done")
        q_doubled = [[sem(f"q_doubled{i}{h}") for h in range(2)] for i in range(2)]
        scores_ready = sem("scores_ready")
        max_done = sem("max_done")
        shift_done = sem("shift_done")
        reloads = sem("reloads")
        ones_made = sem("ones_made")
        exp_done = sem("exp_done")
        turned = sem("turned")
        pt_hi_done = sem("pt_hi_done")
        pt_lo_done = sem("pt_lo_done")
        pv_sum = sem("pv_sum")
        inv_done = sem("inv_done")
        wide_done = sem("wide_done")
        spread_sum = sem("spread_sum")
        spread_done = sem("spread_done")
        o_done = sem("o_done")
        o_hi_done = sem("o_hi_done")
        o_lo_done = sem("o_lo_done")
        proj_sum = sem("proj_sum")
        proj_done = sem("proj_done")
        stats_done = sem("stats_done")
        proj_stored = [sem(f"proj_stored{i}") for i in range(2)]

        w_in = (probs.rearrange("p u (h n) -> p (u h) n", h=NR // C),
                pt_lo[:, 1].bitcast(F32).rearrange("p h t n -> p (h t n)").rearrange("p (ct n) -> p ct n", n=C))
        TERMS = ((wq_hi, x_hi), (wq_lo, x_hi), (wq_hi, x_lo))

        def tile_at(c, gi):
            return (c - 1, gi // 2 - 1) if gi else (c - 2, CT - 1)

        def x_load(sp, c):
            wait(sp, x_lo_done, CT * c)
            sp.dma_start(x_in[:, :, :], x_chunks[c // NCH, c % NCH]
                         ).then_inc(x0_landed if isinstance(c, int) and c == 0 else x_landed, 16)

        def k_load(sp, b, p):
            for h in (2 * p, 2 * p + 1):
                sp.dma_start(k_sb[:, h, :].bitcast(F32), k_scr[b, h].rearrange("s d m -> (s d) m")
                             ).then_inc(k_landed[p], 16)

        def v_load(sp, b, p):
            cols = slice(p * P, (p + 1) * P)
            for part, dst in enumerate((vh_sb, vl_sb)):
                sp.dma_start(dst[:, :, cols], v_scr[b, part, :, :, cols].rearrange("t m c -> m t c")
                             ).then_inc(v_landed[p], 16)
            sp.dma_start(f_sb[:, p, :], f_scr[b]).then_inc(v_landed[p], 16)

        def q_double(sp, pair, par):
            for hh in range(2):
                own, other = slice(hh * DK, (hh + 1) * DK), slice((1 - hh) * DK, (2 - hh) * DK)
                sp.wait_ge(q_lo_done, 2 * pair + hh + 1)
                sp.dma_start(q_x[other, par, hh, :].bitcast(F32), q_y[own, par, hh, :].bitcast(F32)
                             ).then_inc(q_doubled[par][hh], 16)
                sp.dma_start(q_y[other, par, hh, :].bitcast(F32), q_x[own, par, hh, :].bitcast(F32)
                             ).then_inc(q_doubled[par][hh], 16)

        with nc.Block() as block:

            @block.sync
            def _(sp):
                x_load(sp, 0)
                for i in range(2 * CT):
                    src = (wq, wp)[i // CT][(i % CT) * P:(i % CT + 1) * P, :]
                    sp.dma_start(w_in[i // CT][:, i % CT, :], src).then_inc(w_landed[i], 16)
                    if i == CT - 1:
                        k_load(sp, 0, 0)
                        sp.dma_start(bias_sb[:, :], bias.to_broadcast([P, NH])).then_inc(bias_landed, 16)
                q_double(sp, 0, 0)
                v_load(sp, 0, 0)
                for p in range(1, CP):
                    k_load(sp, 0, p)
                    v_load(sp, 0, p)

                def chunk(c, first_of_image=False, last_of_image=False):
                    for gi in range(CG):
                        if gi % 2 == 0:
                            cc, mo = tile_at(c, gi)
                            if there(cc * CT + mo, TILES):
                                sp.wait_ge(proj_done, cc * CT + mo + 1)
                                sp.dma_start(p_scr[cc, mo], proj[:, mo % 2, :]
                                             ).then_inc(proj_stored[mo % 2], 16)
                        else:
                            pair = CP * c + (gi + 1) // 2
                            if there(pair, PAIRS):
                                q_double(sp, pair, (gi + 1) // 2 % 2)
                        if gi == 3 and there(c + 1, CHUNKS):
                            x_load(sp, c + 1)
                        if last_of_image and gi in (2, 4, 6):
                            p = gi // 2 - 1
                            sp.wait_ge(scores_ready, CU * c + NH * (p + 1))
                            sp.sem_inc(reloads, 1)
                            k_load(sp, (c + 1) // NCH, p)
                        if last_of_image and gi in (3, 5, 7):
                            p = (gi - 3) // 2
                            sp.wait_ge(o_done, CG * c + 2 * p + 2)
                            sp.sem_inc(reloads, 1)
                            v_load(sp, (c + 1) // NCH, p)
                        if first_of_image and gi == 0:
                            sp.wait_ge(scores_ready, CU * c)
                            sp.sem_inc(reloads, 1)
                            k_load(sp, c // NCH, CP - 1)
                        if first_of_image and gi == 1:
                            sp.wait_ge(o_done, CG * c)
                            sp.sem_inc(reloads, 1)
                            v_load(sp, c // NCH, CP - 1)

                if B > 1:
                    chunk(0)
                    chunk(1)
                    with sp.Fori(2, NCH - 1) as c:
                        chunk(c)
                    chunk(NCH - 1, last_of_image=True)
                if B > 2:
                    with sp.Fori(1, B - 1) as b:
                        chunk(b * NCH, first_of_image=True)
                        with sp.Fori(1, NCH - 1) as j:
                            chunk(b * NCH + j)
                        chunk(b * NCH + NCH - 1, last_of_image=True)
                last = (B - 1) * NCH
                chunk(last, first_of_image=B > 1)
                chunk(last + 1)
                with sp.Fori(last + 2, CHUNKS - 1) as c:
                    chunk(c)
                for c in (CHUNKS - 1, CHUNKS, CHUNKS + 1):
                    chunk(c)
                for s in range(2):
                    sp.wait_ge(proj_stored[s], 16 * TILES // 2)

            @block.tensor
            def _(pe):
                def o_proj(cc, mo, half):
                    wait(pe, proj_done, cc * CT + mo)
                    pe.wait_ge(w_lo_done, 2 * CT)
                    for kt in (2 * half, 2 * half + 1):
                        pe.wait_ge(o_lo_done, CG * cc + 2 * kt + 2)
                        for n, (w, a) in enumerate(((wp_hi, o_hi), (wp_lo, o_hi), (wp_hi, o_lo))):
                            mm = nc.tensor.matmul(g_ps[:, :], w[:, kt, mo * P:(mo + 1) * P],
                                                  a[:, cc % 2, kt, :],
                                                  start=(kt == 0 and n == 0), stop=(kt == CT - 1 and n == 2))
                    if half:
                        mm.then_inc(proj_sum, 1)

                def q_half(c, p, half):
                    for ct in (2 * half, 2 * half + 1):
                        pe.wait_ge(x_lo_done, CT * c + ct + 1)
                        for n, (w, a) in enumerate(TERMS):
                            mm = nc.tensor.matmul(g_ps[:, :], w[:, ct, p * P:(p + 1) * P], a[:, ct, :],
                                                  start=(ct == 0 and n == 0), stop=(ct == CT - 1 and n == 2))
                    if half:
                        mm.then_inc(q_sum, 1)

                def scores(c, gi, k):
                    unit, p, hh, nt = CU * c + 4 * gi + k, gi // 2, k // 2, 2 * (gi % 2) + k % 2
                    if gi % 2 == 0 and k == 0:
                        pe.wait_ge(k_landed[p], 32 * (c // NCH) + 32)
                    if gi % 2 == 0 and k % 2 == 0:
                        pe.wait_ge(q_doubled[p % 2][hh], 32 * (CP * c // 2 + p // 2) + 32)
                    wait(pe, exp_done, unit - 1)
                    ps = s_ps[k % 2]
                    for n, q in enumerate((q_x, q_y)):
                        for m in range(NR // CH):
                            mm = nc.tensor.matmul(ps[:, m * CH:(m + 1) * CH],
                                                  q[:, p % 2, hh, nt * P:(nt + 1) * P],
                                                  k_sb[:, 2 * p + hh, m * CH:(m + 1) * CH],
                                                  start=(n == 0), stop=(n == 1))
                    mm.then_inc(scores_ready, 1)

                def turn(unit, k):
                    pe.wait_ge(exp_done, unit + 1)
                    for half in range(2):
                        wait(pe, pt_lo_done, 2 * unit - 1 + half)
                        for i in range(MT // 2):
                            m = half * (MT // 2) + i
                            mm = nc.tensor.transpose(t_ps[half][:, i * P:(i + 1) * P],
                                                     probs[:, k % 2, m * P:(m + 1) * P], ident[:, :])
                        mm.then_inc(turned, 1)

                def pv(c, gi, part):
                    group, p = CG * c + gi, gi // 2
                    if part == 0:
                        pe.wait_ge(v_landed[p], 48 * (c // NCH) + 48)
                        pe.wait_ge(pt_lo_done, 8 * group + 8)
                        wait(pe, o_done, group)
                    for mt in range(part * MT // 2, (part + 1) * MT // 2):
                        for n, (v, pt) in enumerate(((vh_sb, pt_hi), (vl_sb, pt_hi), (vh_sb, pt_lo))):
                            for hh in range(2):
                                own = slice(hh * DK, (hh + 1) * DK)
                                mm = nc.tensor.matmul(
                                    pv_ps[own, 0:HALF], v[:, mt, (2 * p + hh) * DK:(2 * p + hh + 1) * DK],
                                    pt[:, gi % 2, hh, mt, :],
                                    start=(mt == 0 and n == 0), stop=(mt == MT - 1 and n == 2),
                                    skip_group_check=True)
                    if part:
                        mm.then_inc(pv_sum, 1)

                def spread_inv(group):
                    pe.wait_ge(wide_done, group + 1)
                    for nt in range(2):
                        mm = nc.tensor.matmul(g_ps[:, nt * P:(nt + 1) * P],
                                              inv_wide[:, nt].rearrange("p h d -> p (h d)"), ident[:, :],
                                              start=True, stop=True)
                    mm.then_inc(spread_sum, 1)

                def chunk(c):
                    for gi in range(CG):
                        group = CG * c + gi
                        cl, gl = (c, gi - 1) if gi else (c - 1, CG - 1)
                        for k in range(4):
                            unit = 4 * group + k
                            if there(unit, UNITS):
                                scores(c, gi, k)
                            if there(unit - 1, UNITS):
                                turn(unit - 1, (k - 1) % 4)
                            if k < 2:
                                if k == 0:
                                    wait(pe, spread_done, group - 1 if there(group - 1, GROUPS + 1) else 0)
                                if gi % 2:
                                    if there(CP * c + (gi + 1) // 2, PAIRS):
                                        q_half(c + (gi == CG - 1), (gi + 1) // 2 % CP, k)
                                else:
                                    cc, mo = tile_at(c, gi)
                                    if there(cc * CT + mo, TILES):
                                        o_proj(cc, mo, k)
                            elif there(group - 1, GROUPS):
                                if k == 3:
                                    if gi % 2:
                                        wait(pe, q_lo_done, 2 * (CP * c + (gi + 1) // 2) + 2 if there(CP * c + (gi + 1) // 2, PAIRS) else 0)
                                    else:
                                        cc, mo = tile_at(c, gi)
                                        wait(pe, proj_done, cc * CT + mo + 1 if there(cc * CT + mo, TILES) else 0)
                                    spread_inv(group - 1)
                                pv(cl, gl, k - 2)

                pe.wait_ge(w_lo_done, CT // 2)
                q_half(0, 0, 0)
                pe.wait_ge(w_lo_done, CT)
                q_half(0, 0, 1)
                for c in range(2):
                    chunk(c)
                with pe.Fori(2, CHUNKS - 1) as c:
                    chunk(c)
                for c in range(CHUNKS - 1, CHUNKS + 2):
                    chunk(c)

            @block.scalar
            def _(act):
                def q_split(pair, par):
                    act.wait_ge(q_sum, pair + 1)
                    wait(act, scores_ready, 8 * (pair - 1))
                    for hh in range(2):
                        own = slice(hh * DK, (hh + 1) * DK)
                        nc.scalar.mul(q_x[own, par, hh, :], g_ps[own, :], SCALE).then_inc(q_hi_done, 1)

                def pt_split(c, gi, k):
                    group = CG * c + gi
                    unit = 4 * group + k
                    if k == 0:
                        wait(act, pv_sum, group - 1)
                    for half in range(2):
                        act.wait_ge(turned, 2 * unit + half + 1)
                        nc.scalar.mul(
                            pt_hi[:, gi % 2, k // 2, half * (MT // 2):(half + 1) * (MT // 2),
                                  (k % 2) * P:(k % 2 + 1) * P],
                            t_ps[half].rearrange("p (t n) -> p t n", n=P), P_SCALE).then_inc(pt_hi_done, 1)

                def exps(c, gi, k):
                    group = CG * c + gi
                    unit = 4 * group + k
                    if k == 0:
                        wait(act, inv_done, group - 1)
                    act.wait_ge(shift_done, unit + 1)
                    wait(act, turned, 2 * unit - 2)
                    nc.scalar.activation(probs[:, k % 2, :], s_ps[k % 2][:, :], ACT.Exp,
                                         bias=shift[:, k % 2:k % 2 + 1],
                                         accum_out=sums[:, gi % 2, k % 2, k // 2:k // 2 + 1]
                                         ).then_inc(exp_done, 1)

                def chunk(c):
                    for gi in range(CG):
                        group = CG * c + gi
                        cl, gl = (c, gi - 1) if gi else (c - 1, CG - 1)
                        c2, g2 = (c, gi - 2) if gi > 1 else (c - 1, gi - 2 + CG)
                        for k in range(4):
                            unit = 4 * group + k
                            if k == 2 and gi % 2 and there(CP * c + (gi + 1) // 2, PAIRS):
                                q_split(CP * c + (gi + 1) // 2, (gi + 1) // 2 % 2)
                            if there(unit - 1, UNITS):
                                pt_split(*((c, gi, k - 1) if k else (cl, gl, 3)))
                            cc, mo = tile_at(c, gi)
                            if k == 2 and gi % 2 == 0 and there(cc * CT + mo, TILES):
                                n = cc * CT + mo
                                act.wait_ge(proj_sum, n + 1)
                                wait(act, stats_done, n - 1)
                                wait(act, proj_stored[mo % 2], 16 * (cc * CT // 2 + mo // 2))
                                nc.scalar.copy(proj[:, mo % 2, :], g_ps[:, :]).then_inc(proj_done, 1)
                            if there(unit, UNITS):
                                exps(c, gi, k)
                            if k == 1 and there(group - 2, GROUPS):
                                act.wait_ge(o_done, group - 1)
                                if g2 == 0:
                                    wait(act, proj_sum, CT * (c2 - 1))
                                nc.scalar.copy(o_hi[:, c2 % 2, g2 // 2, (gi % 2) * HALF:(gi % 2 + 1) * HALF],
                                               o_sb[:, gi % 2, :]).then_inc(o_hi_done, 1)
                            if k == 3 and there(group - 1, GROUPS):
                                act.wait_ge(spread_sum, group)
                                wait(act, o_done, group - 1)
                                nc.scalar.copy(spread[:, :], g_ps[:, 0:HALF]).then_inc(spread_done, 1)

                for i in range(2 * CT):
                    if i == 0:
                        act.wait_ge(x0_landed, 16)
                    if i == CT:
                        q_split(0, 0)
                    if i < CT:
                        nc.scalar.copy(x_hi[:, i, :], x_in[:, i, :]).then_inc(x_hi_done, 1)
                    act.wait_ge(w_landed[i], 16)
                    nc.scalar.copy((wq_hi, wp_hi)[i // CT][:, i % CT, :], w_in[i // CT][:, i % CT, :]
                                   ).then_inc(w_hi_done, 1)
                for c in range(2):
                    chunk(c)
                with act.Fori(2, CHUNKS - 1) as c:
                    chunk(c)
                for c in range(CHUNKS - 1, CHUNKS + 2):
                    chunk(c)

            @block.vector
            def _(dve):
                def q_split(pair, par):
                    for hh in range(2):
                        own = slice(hh * DK, (hh + 1) * DK)
                        dve.wait_ge(q_hi_done, 2 * pair + hh + 1)
                        nc.vector.scalar_tensor_tensor(out=q_y[own, par, hh, :], in0=g_ps[own, :], scalar=SCALE,
                                                       in1=q_x[own, par, hh, :], op0=ALU.mult,
                                                       op1=ALU.subtract).then_inc(q_lo_done, 1)

                def pt_split(c, gi, k):
                    unit = CU * c + 4 * gi + k
                    for half in range(2):
                        dve.wait_ge(pt_hi_done, 2 * unit + half + 1)
                        at = (slice(None), gi % 2, k // 2, slice(half * (MT // 2), (half + 1) * (MT // 2)),
                              slice((k % 2) * P, (k % 2 + 1) * P))
                        nc.vector.scalar_tensor_tensor(out=pt_lo[at], in0=t_ps[half].rearrange("p (t n) -> p t n", n=P),
                                                       scalar=P_SCALE, in1=pt_hi[at], op0=ALU.mult,
                                                       op1=ALU.subtract).then_inc(pt_lo_done, 1)

                def chunk(c):
                    for gi in range(CG):
                        group = CG * c + gi
                        cl, gl = (c, gi - 1) if gi else (c - 1, CG - 1)
                        c2, g2 = (c, gi - 2) if gi > 1 else (c - 1, gi - 2 + CG)
                        for k in range(4):
                            unit = 4 * group + k
                            if there(unit, UNITS):
                                dve.wait_ge(scores_ready, unit + 1)
                                wait(dve, exp_done, unit - 1)
                                nc.vector.tensor_reduce(neg_max[:, k % 2:k % 2 + 1], s_ps[k % 2][:, :], AX.X,
                                                        ALU.max, negate=True).then_inc(max_done, 1)
                                h = 2 * (gi // 2) + k // 2
                                dve.wait_ge(max_done, unit + 1)
                                nc.vector.tensor_scalar(shift[:, k % 2:k % 2 + 1], neg_max[:, k % 2:k % 2 + 1],
                                                        bias_sb[:, h:h + 1], bias_sb[:, h:h + 1],
                                                        ALU.subtract, ALU.add).then_inc(shift_done, 1)
                            if k == 0 and there(group - 2, GROUPS):
                                dve.wait_ge(pv_sum, group - 1)
                                dve.wait_ge(spread_done, group - 1)
                                wait(dve, o_lo_done, group - 3)
                                nc.vector.scalar_tensor_tensor(
                                    out=o_sb[:, gi % 2, :], in0=pv_ps[:, 0:HALF],
                                    scalar=f_sb[:, g2 // 2, g2 // 2:g2 // 2 + 1], in1=spread[:, :],
                                    op0=ALU.mult, op1=ALU.mult).then_inc(o_done, 1)
                            if k == 1 and there(group - 1, GROUPS):
                                dve.wait_ge(exp_done, 4 * group)
                                wait(dve, wide_done, group - 1)
                                nc.vector.reciprocal(inv[:, :, :], sums[:, gl % 2, :, :]).then_inc(inv_done, 1)
                            if k == 2 and gi % 2 and there(CP * c + (gi + 1) // 2, PAIRS):
                                q_split(CP * c + (gi + 1) // 2, (gi + 1) // 2 % 2)
                            if there(unit - 1, UNITS):
                                pt_split(*((c, gi, k - 1) if k else (cl, gl, 3)))
                            cc, mo = tile_at(c, gi)
                            if k == 3 and gi % 2 == 0 and there(cc * CT + mo, TILES):
                                dve.wait_ge(proj_done, cc * CT + mo + 1)
                                nc.vector.bn_stats(stats[:, mo, cc, :], proj[:, mo % 2, :]).then_inc(stats_done, 1)

                for i in range(2 * CT):
                    if i == CT:
                        q_split(0, 0)
                    if i < CT:
                        dve.wait_ge(x_hi_done, i + 1)
                        nc.vector.tensor_tensor(x_lo[:, i, :], x_in[:, i, :], x_hi[:, i, :], ALU.subtract
                                                ).then_inc(x_lo_done, 1)
                    dve.wait_ge(w_hi_done, i + 1)
                    nc.vector.tensor_tensor((wq_lo, wp_lo)[i // CT][:, i % CT, :], w_in[i // CT][:, i % CT, :],
                                            (wq_hi, wp_hi)[i // CT][:, i % CT, :], ALU.subtract).then_inc(w_lo_done, 1)
                dve.wait_ge(bias_landed, 16)
                for c in range(2):
                    chunk(c)
                with dve.Fori(2, CHUNKS - 1) as c:
                    chunk(c)
                for c in range(CHUNKS - 1, CHUNKS + 2):
                    chunk(c)

            @block.gpsimd
            def _(pool):
                def x_split(c, ct):
                    if ct == 0:
                        pool.wait_ge(x_landed, 16 * c)
                        wait(pool, q_sum, CP * c)
                    nc.gpsimd.tensor_tensor(x_hi[:, ct, :].rearrange("p (i n) -> p i n", n=P),
                                            x_in[:, ct, :].rearrange("p (i n) -> p i n", n=P),
                                            ones.rearrange("p (o n) -> p o n", o=1).to_broadcast([P, CH // P, P]),
                                            ALU.mult).then_inc(x_hi_done, 1)
                    pool.wait_ge(x_hi_done, CT * c + ct + 1)
                    nc.gpsimd.tensor_tensor(x_lo[:, ct, :], x_in[:, ct, :], x_hi[:, ct, :], ALU.subtract
                                            ).then_inc(x_lo_done, 1)

                def chunk(c):
                    for gi in range(CG):
                        group = CG * c + gi
                        c2, g2 = (c, gi - 2) if gi > 1 else (c - 1, gi - 2 + CG)
                        for k in range(4):
                            if k == 1 and there(group - 1, GROUPS):
                                pool.wait_ge(inv_done, group)
                                wait(pool, spread_sum, group - 1)
                                for nt in range(2):
                                    last = nc.gpsimd.tensor_tensor(
                                        inv_wide[:, nt], inv[:, nt, :].unsqueeze(2).to_broadcast([P, 2, DK]),
                                        ones.rearrange("p (h d) -> p h d", d=DK), ALU.mult)
                                last.then_inc(wide_done, 1)
                            if k == 2 and there(group - 2, GROUPS):
                                pool.wait_ge(o_hi_done, group - 1)
                                at = (slice(None), c2 % 2, g2 // 2, slice((gi % 2) * HALF, (gi % 2 + 1) * HALF))
                                nc.gpsimd.tensor_tensor(o_lo[at], o_sb[:, gi % 2, :], o_hi[at], ALU.subtract
                                                        ).then_inc(o_lo_done, 1)
                            if gi == 6 and there(c + 1, CHUNKS):
                                x_split(c + 1, k)

                nc.gpsimd.memset(ones[:, :], 1.0).then_inc(ones_made, 1)
                pool.wait_ge(ones_made, 1)
                for c in range(2):
                    chunk(c)
                with pool.Fori(2, CHUNKS - 1) as c:
                    chunk(c)
                for c in range(CHUNKS - 1, CHUNKS + 2):
                    chunk(c)


def norms(nc, x_chunks, out_chunks, p_scr, stats, bn_gamma, bn_beta, ln_gamma, ln_beta,
          B, C, CT, CH, NCH):
    CHUNKS = B * NCH
    with ExitStack() as ctx:
        def sb(name, shape, dt=F32):
            return ctx.enter_context(nc.sbuf_tensor(name, shape, dt))

        def sem(name):
            return ctx.enter_context(nc.semaphore(name))

        vecs = sb("vecs", [P, 4, CT])
        moments = sb("moments", [P, CT, 2])
        std = sb("std", [P, CT])
        rstd = sb("rstd", [P, CT])
        eps = sb("eps", [P, 1])
        a_bn = sb("a_bn", [P, CT])
        ma = sb("ma", [P, CT])
        b_bn = sb("b_bn", [P, CT])
        mean_w = sb("mean_w", [P, P])
        x_in = sb("x3_in", [P, 4, CT, CH])
        p_in = sb("p3_in", [P, 4, CT, CH])
        bn = sb("bn", [P, 2, CT, CH])
        y = sb("y", [P, 2, CT, CH])
        d = sb("d", [P, 4, CT, CH])
        sq = sb("sq", [P, 2, CT, CH])
        dev = sb("dev", [P, 2, CH])
        ln = sb("ln", [P, 2, CH])
        z = sb("z", [P, 2, CT, CH])
        o = sb("o", [P, 2, CT, CH])
        mean_ps = [ctx.enter_context(nc.psum_tensor(f"mean_ps{i}", [P, CH], F32)) for i in range(2)]
        var_ps = [ctx.enter_context(nc.psum_tensor(f"var_ps{i}", [P, CH], F32)) for i in range(2)]

        vecs_landed = sem("vecs_landed")
        w_done = sem("mean_w_done")
        coef = sem("coef")
        std_done = sem("std_done")
        x_landed = [sem(f"x3_landed{i}") for i in range(4)]
        p_landed = [sem(f"p3_landed{i}") for i in range(4)]
        bn_done = sem("bn_done")
        y_done = sem("y_done")
        mean_done = sem("mean_done")
        d_done = sem("d_done")
        sq_done = sem("sq_done")
        var_done = sem("var_done")
        dev_done = sem("dev_done")
        ln_done = sem("ln_done")
        z_done = sem("z_done")
        o_done = sem("o3_done")
        stored = [sem(f"stored{i}") for i in range(2)]
        COEFS = CT + 4

        assert CHUNKS % 4 == 0 and CHUNKS >= 12

        def run(eng, step, extra):
            for s in range(8):
                step(s, s % 4, s // 4)
            with eng.Fori(2, CHUNKS // 4 - 1) as u:
                for j in range(4):
                    step(u * 4 + j, j, u)
            for s in range(CHUNKS - 4, CHUNKS + extra):
                step(s, s % 4, s // 4)

        with nc.Block() as block:

            @block.sync
            def _(sp):
                for i, v in enumerate((bn_gamma, bn_beta, ln_gamma, ln_beta)):
                    sp.dma_start(vecs[:, i, :], v).then_inc(vecs_landed, 16)

                def load(s, j):
                    wait(sp, bn_done, s - 3)
                    sp.dma_start(p_in[:, j], p_scr[s].rearrange("ct p n -> p ct n")).then_inc(p_landed[j], 16)
                    wait(sp, y_done, s - 3)
                    sp.dma_start(x_in[:, j], x_chunks[s // NCH, s % NCH]).then_inc(x_landed[j], 16)

                def step(s, j, u):
                    if there(s + 2, CHUNKS):
                        load(s + 2, (j + 2) % 4)
                    if there(s - 4, CHUNKS):
                        sp.wait_ge(o_done, s - 3)
                        sp.dma_start(out_chunks[(s - 4) // NCH, (s - 4) % NCH], o[:, j % 2]).then_inc(stored[j % 2], 16)
                load(0, 0)
                load(1, 1)
                run(sp, step, 4)
                for j in range(2):
                    sp.wait_ge(stored[j], 16 * CHUNKS // 2)

            @block.scalar
            def _(act):
                act.wait_ge(w_done, 2)
                act.wait_ge(coef, CT)
                nc.scalar.activation(std[:, :], moments[:, :, 1], ACT.Sqrt, bias=eps[:, :]).then_inc(std_done, 1)
                act.wait_ge(coef, COEFS)
                act.wait_ge(vecs_landed, 64)

                def step(s, j, u):
                    if there(s, CHUNKS):
                        act.wait_ge(p_landed[j], 16 * u + 16)
                        wait(act, y_done, s - 1)
                        for ct in range(CT):
                            last = nc.scalar.activation(bn[:, j % 2, ct], p_in[:, j, ct], ACT.Identity,
                                                        bias=b_bn[:, ct:ct + 1], scale=a_bn[:, ct:ct + 1])
                        last.then_inc(bn_done, 1)
                    if there(s - 3, CHUNKS):
                        act.wait_ge(var_done, s - 2)
                        wait(act, ln_done, s - 4)
                        nc.scalar.activation(dev[:, (j + 1) % 2], var_ps[(j + 1) % 2][:, :], ACT.Sqrt,
                                             bias=eps[:, :]).then_inc(dev_done, 1)
                    if there(s - 2, CHUNKS):
                        act.wait_ge(d_done, s - 1)
                        wait(act, var_done, s - 3)
                        nc.scalar.activation(sq[:, j % 2], d[:, (j + 2) % 4], ACT.Square).then_inc(sq_done, 1)
                    if there(s - 4, CHUNKS):
                        act.wait_ge(z_done, s - 3)
                        wait(act, stored[j % 2], 16 * (2 * u + j // 2 - 2))
                        for ct in range(CT):
                            last = nc.scalar.activation(o[:, j % 2, ct], z[:, j % 2, ct], ACT.Identity,
                                                        bias=vecs[:, 3, ct:ct + 1], scale=vecs[:, 2, ct:ct + 1])
                        last.then_inc(o_done, 1)
                run(act, step, 4)

            @block.gpsimd
            def _(pool):
                nc.gpsimd.memset(mean_w[:, :], 1.0 / C).then_inc(w_done, 1)
                nc.gpsimd.memset(eps[:, :], EPS).then_inc(w_done, 1)

                def step(s, j, u):
                    pool.wait_ge(bn_done, s + 1)
                    pool.wait_ge(x_landed[j], 16 * u + 16)
                    wait(pool, d_done, s - 1)
                    wait(pool, mean_done, s - 1)
                    nc.gpsimd.tensor_tensor(y[:, j % 2], x_in[:, j], bn[:, j % 2], ALU.add).then_inc(y_done, 1)
                run(pool, step, 0)

            @block.tensor
            def _(pe):
                pe.wait_ge(w_done, 2)

                def step(s, j, u):
                    i = (j + 1) % 2
                    if there(s - 1, CHUNKS):
                        pe.wait_ge(y_done, s)
                        wait(pe, d_done, s - 2)
                        for ct in range(CT):
                            mm = nc.tensor.matmul(mean_ps[i][:, :], mean_w[:, :], y[:, i, ct],
                                                  start=(ct == 0), stop=(ct == CT - 1))
                        mm.then_inc(mean_done, 1)
                    if there(s - 2, CHUNKS):
                        pe.wait_ge(sq_done, s - 1)
                        wait(pe, dev_done, s - 3)
                        for ct in range(CT):
                            mm = nc.tensor.matmul(var_ps[j % 2][:, :], mean_w[:, :], sq[:, j % 2, ct],
                                                  start=(ct == 0), stop=(ct == CT - 1))
                        mm.then_inc(var_done, 1)
                run(pe, step, 2)

            @block.vector
            def _(dve):
                for ct in range(CT):
                    nc.vector.bn_aggr(moments[:, ct, :], stats[:, ct].rearrange("p c s -> p (c s)")).then_inc(coef, 1)
                dve.wait_ge(coef, CT)
                dve.wait_ge(vecs_landed, 64)
                dve.wait_ge(std_done, 1)
                nc.vector.reciprocal(rstd[:, :], std[:, :]).then_inc(coef, 1)
                dve.wait_ge(coef, CT + 1)
                nc.vector.tensor_tensor(a_bn[:, :], rstd[:, :], vecs[:, 0], ALU.mult).then_inc(coef, 1)
                dve.wait_ge(coef, CT + 2)
                nc.vector.tensor_tensor(ma[:, :], moments[:, :, 0], a_bn[:, :], ALU.mult).then_inc(coef, 1)
                dve.wait_ge(coef, CT + 3)
                nc.vector.tensor_tensor(b_bn[:, :], vecs[:, 1], ma[:, :], ALU.subtract).then_inc(coef, 1)

                def step(s, j, u):
                    i = (j + 1) % 2
                    if there(s - 3, CHUNKS):
                        dve.wait_ge(dev_done, s - 2)
                        wait(dve, z_done, s - 4)
                        nc.vector.reciprocal(ln[:, i, :], dev[:, i, :]).then_inc(ln_done, 1)
                        dve.wait_ge(ln_done, s - 2)
                        wait(dve, o_done, s - 4)
                        nc.vector.tensor_tensor(z[:, i], d[:, (j + 1) % 4],
                                                ln[:, i, :].unsqueeze(1).to_broadcast([P, CT, CH]),
                                                ALU.mult).then_inc(z_done, 1)
                    if there(s - 1, CHUNKS):
                        dve.wait_ge(mean_done, s)
                        wait(dve, sq_done, s - 4)
                        wait(dve, z_done, s - 4)
                        nc.vector.tensor_tensor(d[:, (j + 3) % 4], y[:, i],
                                                mean_ps[i][:, :].unsqueeze(1).to_broadcast([P, CT, CH]),
                                                ALU.subtract).then_inc(d_done, 1)
                run(dve, step, 3)


def kernel(x, L0_conv_Wq, L0_conv_Wk, L0_conv_Wv, L0_conv_bias, L0_conv_Wproj, L0_conv_bn_gamma,
           L0_conv_bn_beta, L0_conv_ln_gamma, L0_conv_ln_beta):
    import numpy as np
    import concourse.bacc as bacc
    from concourse.bass_utils import run_bass_kernel_spmd

    def pointwise(w):
        return np.ascontiguousarray(np.asarray(w)[:, :, 0, 0].T)

    def taps(w):
        w = np.asarray(w)
        return np.ascontiguousarray(w.transpose(1, 2, 3, 0).reshape(w.shape[1], -1, w.shape[0]))

    def column(v):
        return np.ascontiguousarray(np.asarray(v).reshape(-1, P).T)

    arrays = {
        "x": np.ascontiguousarray(x),
        "wq": pointwise(L0_conv_Wq),
        "wk": taps(L0_conv_Wk),
        "wv": taps(L0_conv_Wv),
        "bias": np.ascontiguousarray(np.asarray(L0_conv_bias).reshape(1, -1)),
        "wp": pointwise(L0_conv_Wproj),
        "bn_gamma": column(L0_conv_bn_gamma),
        "bn_beta": column(L0_conv_bn_beta),
        "ln_gamma": column(L0_conv_ln_gamma),
        "ln_beta": column(L0_conv_ln_beta),
    }
    nc = bacc.Bacc("TRN2", target_bir_lowering=False, num_devices=1)
    args = [nc.dram_tensor(n, a.shape, mybir.dt.from_np(a.dtype), kind="ExternalInput").ap()
            for n, a in arrays.items()]
    out = nc.dram_tensor("out", arrays["x"].shape, F32, kind="ExternalOutput").ap()
    conv_attention(nc, *args, out)
    return run_bass_kernel_spmd(nc, [arrays], core_ids=[0]).results[0]["out"]
```

```python
from contextlib import ExitStack

import concourse.bass as bass
from concourse import mybir

ALU = mybir.AluOpType
ACT = mybir.ActivationFunctionType
AX = mybir.AxisListType
F32 = mybir.dt.float32
F32R = mybir.dt.float32r
F16 = mybir.dt.float16

P = 128
NH = 8
R = 2
RS = R * R
EPS = 1e-5
P_SCALE = 4096.0
V_SCALE = 1024.0
TINY = 1e-30


def wait(eng, semaphore, value):
    if not isinstance(value, int) or value > 0:
        eng.wait_ge(semaphore, value)


def there(i, n):
    return not isinstance(i, int) or 0 <= i < n


def conv_attention(nc, x, wq, wk, wv, bias, wp, bn_gamma, bn_beta, ln_gamma, ln_beta, out):
    B, C, H, W = x.shape
    CT = C // P
    DK = C // NH
    NR = H * W // RS
    CH = 512
    NCH = H * W // CH
    MT = NR // P
    ROWS = CH // W
    assert NCH == MT and CH // RS == P and DK * 2 == P

    k_scr = nc.dram_tensor("k_scr", (B, NH, 2, DK, NR), F32, kind="Internal").ap()
    v_scr = nc.dram_tensor("v_scr", (B, CT, P, MT, 2, P), F16, kind="Internal").ap()
    f_scr = nc.dram_tensor("f_scr", (B, P, CT), F32, kind="Internal").ap()
    p_scr = nc.dram_tensor("p_scr", (B * NCH, CT, P, CH), F32, kind="Internal").ap()

    x_chunks = x.rearrange("b (ct p) (t r) w -> b t p ct (r w)", p=P, r=ROWS)
    out_chunks = out.rearrange("b (ct p) (t r) w -> b t p ct (r w)", p=P, r=ROWS)

    with ExitStack() as whole:
        ident = whole.enter_context(nc.sbuf_tensor("ident", [P, P], F32))
        stats = whole.enter_context(nc.sbuf_tensor("stats", [P, CT, B * NCH, 6], F32))
        keys_and_values(nc, x_chunks, wk, wv, ident, k_scr, v_scr, f_scr, B, C, CT, MT, CH, W)
        attention(nc, x_chunks, wq, wp, bias, ident, stats, k_scr, v_scr, f_scr, p_scr,
                  B, C, CT, NR, MT, CH, NCH, DK)
        norms(nc, x_chunks, out_chunks, p_scr, stats, bn_gamma, bn_beta, ln_gamma, ln_beta,
              B, C, CT, CH, NCH)


def keys_and_values(nc, x_chunks, wk, wv, ident, k_scr, v_scr, f_scr, B, C, CT, MT, CH, W):
    DK = C // NH
    KT = CT * RS
    VB = 4
    SLICES = 2 * KT
    with ExitStack() as ctx:
        def sb(name, shape, dt=F32):
            return ctx.enter_context(nc.sbuf_tensor(name, shape, dt))

        def psum(name):
            return ctx.enter_context(nc.psum_tensor(name, [P, CH], F32))

        def sem(name):
            return ctx.enter_context(nc.semaphore(name))

        w_hi = sb("w_hi", [P, SLICES, C], F32R)
        w_lo = sb("w_lo", [P, SLICES, C], F32R)
        x_in = sb("x1_in", [P, CT, CH])
        x_hi = sb("x1_hi", [P, 2, CT, RS, P], F32R)
        x_lo = sb("x1_lo", [P, 2, CT, RS, P], F32R)
        v_all = sb("v_all", [P, MT, C])
        k_nat = sb("k_nat", [P, C])
        k_hi = sb("k_hi", [P, CT, P], F32R)
        k_lo = sb("k_lo", [P, CT, P], F32R)
        v_parts = sb("v_parts", [P, VB, CT, 2, P], F16)
        v_abs = sb("v_abs", [P, C])
        v_row = sb("v_row", [P, C])
        v_max = sb("v_max", [P, CT])
        v_div = sb("v_div", [P, CT])
        v_inv = sb("v_inv", [P, CT])
        v_fac = sb("v_fac", [P, CT])
        ones = sb("ones1", [P, P])

        k_ps = [psum(f"k_ps{i}") for i in range(2)]
        v_ps = [psum(f"v_ps{i}") for i in range(2)]
        t_ps = psum("t_ps")
        m_ps = psum("m_ps")

        consts = sem("consts1")
        w_landed = [sem(f"w_landed{i}") for i in range(MT)]
        w_hi_done = sem("w_hi_done")
        w_lo_done = sem("w_lo_done")
        x0_landed = [sem(f"x1_first_landed{ct}") for ct in range(CT)]
        x_landed = sem("x1_landed")
        x_hi_done = sem("x1_hi_done")
        x_lo_done = sem("x1_lo_done")
        k_sum = sem("k_sum")
        v_sum = sem("v_sum")
        k_copied = sem("k_copied")
        v_copied = sem("v_copied")
        k_turned = sem("k_turned")
        k_hi_done = sem("k_hi_done")
        k_lo_done = sem("k_lo_done")
        k_stored = sem("k_stored")
        abs_steps = sem("abs_steps")
        abs_done = sem("abs_done")
        abs_turned = sem("abs_turned")
        vmax_steps = sem("vmax_steps")
        vdiag_done = sem("vdiag_done")
        vrow_sum = sem("vrow_sum")
        vrow_done = sem("vrow_done")
        v_scaled = sem("v_scaled")
        v_hi_done = sem("v_hi_done")
        v_lo_done = sem("v_lo_done")
        v_stored = [sem(f"v_stored{i}") for i in range(VB)]
        f_stored = sem("f_stored")

        x_taps = x_in.rearrange("p ct (i r j s) -> p ct r s i j", r=R, s=R, j=W // R)
        k_dst = k_scr.rearrange("b (ct hh) s d (t m) -> b s hh t d ct m", hh=2, m=P)

        def tiles(v):
            return v.rearrange("p (ct c) -> p ct c", c=P)

        with nc.Block() as block:

            @block.sync
            def _(sp):
                for ct in range(CT):
                    sp.dma_start(x_in[:, ct, :], x_chunks[0, 0, :, ct]).then_inc(x0_landed[ct], 16)
                for i in range(SLICES):
                    kt = i % KT
                    if i >= MT:
                        sp.wait_ge(w_lo_done, i - MT + 1)
                    src = (wk, wv)[i // KT][(kt // RS) * P:(kt // RS + 1) * P, kt % RS, :]
                    sp.dma_start(v_all[:, i % MT, :], src).then_inc(w_landed[i % MT], 16)
                with sp.Fori(1, MT) as i:
                    sp.wait_ge(x_lo_done, i + 1)
                    sp.dma_start(x_in[:, :, :], x_chunks[0, i]).then_inc(x_landed, 16)
                with sp.Fori(1, B) as b:
                    with sp.Fori(0, MT) as i:
                        sp.wait_ge(x_lo_done, b * MT + i + 1)
                        sp.dma_start(x_in[:, :, :], x_chunks[b, i]).then_inc(x_landed, 16)

            @block.gpsimd
            def _(pool):
                nc.gpsimd.memset(ident[:, :], 0.0).then_inc(consts, 1)
                nc.gpsimd.memset(ones[:, :], 1.0).then_inc(consts, 1)
                pool.wait_ge(consts, 2)
                nc.gpsimd.affine_select(out=ident[:, :], in_=ident[:, :], compare_op=ALU.not_equal,
                                        fill=1.0, base=0, pattern=[[-1, P]],
                                        channel_multiplier=1).then_inc(consts, 1)
                pool.sem_inc(x_lo_done, 1)
                pool.sem_inc(x_landed, 16)
                for ct in range(CT):
                    pool.wait_ge(x0_landed[ct], 16)

                def patch(x, j, ct, r):
                    return x[:, j, ct, R * r:R * r + R, :].rearrange("p s (i j) -> p s i j", j=W // R)

                times_one = ones.rearrange("p (s i j) -> p s i j", s=1, j=W // R
                                           ).to_broadcast([P, R, R * P // W, W // R])
                with pool.Fori(0, B * MT // 2) as u:
                    for j in range(2):
                        t = u * 2 + j
                        pool.wait_ge(x_landed, 16 * t + 16)
                        pool.wait_ge(v_sum, t + 1)
                        for ct in range(CT):
                            for r in range(R):
                                last = nc.gpsimd.tensor_tensor(patch(x_hi, j, ct, r), x_taps[:, ct, r], times_one,
                                                               ALU.mult)
                        last.then_inc(x_hi_done, 1)
                        pool.wait_ge(x_hi_done, t + 1)
                        for ct in range(CT):
                            for r in range(R):
                                last = nc.gpsimd.tensor_tensor(patch(x_lo, j, ct, r), x_taps[:, ct, r],
                                                               patch(x_hi, j, ct, r), ALU.subtract)
                        last.then_inc(x_lo_done, 1)

            @block.tensor
            def _(pe):
                pe.sem_inc(v_sum, 2)
                pe.sem_inc(k_turned, 1)
                pe.sem_inc(vrow_sum, 1)
                pe.wait_ge(consts, 3)
                with pe.Fori(0, B) as b:
                    with pe.Fori(0, MT // 2) as u:
                        for j in range(2):
                            t = b * MT + u * 2 + j
                            pe.wait_ge(x_lo_done, t + 2)
                            for kv, (ps, copied, done) in enumerate(((k_ps, k_copied, k_sum),
                                                                     (v_ps, v_copied, v_sum))):
                                pe.wait_ge(copied, t + 1)
                                for kt in range(KT):
                                    if kt % 2 == 0:
                                        pe.wait_ge(w_lo_done, kv * KT + kt + 2)
                                    hi = x_hi[:, j, kt // RS, kt % RS, :]
                                    lo = x_lo[:, j, kt // RS, kt % RS, :]
                                    for n, (a, w) in enumerate(((hi, w_hi), (hi, w_lo), (lo, w_hi))):
                                        mm = nc.tensor.matmul(ps[j][:, :], a, w[:, kv * KT + kt, :],
                                                              start=(kt == 0 and n == 0),
                                                              stop=(kt == KT - 1 and n == 2))
                                mm.then_inc(done, 1)
                            pe.wait_ge(k_copied, t + 3)
                            pe.wait_ge(k_lo_done, t + 1)
                            for ct in range(CT):
                                mm = nc.tensor.transpose(t_ps[:, ct * P:(ct + 1) * P],
                                                         k_nat[:, ct * P:(ct + 1) * P], ident[:, :])
                            mm.then_inc(k_turned, 1)
                    pe.wait_ge(abs_done, b + 1)
                    pe.wait_ge(vrow_done, b + 1)
                    for ct in range(CT):
                        mm = nc.tensor.transpose(m_ps[:, ct * P:(ct + 1) * P],
                                                 v_abs[:, ct * P:(ct + 1) * P], ident[:, :])
                    mm.then_inc(abs_turned, 1)
                    pe.wait_ge(vdiag_done, b + 1)
                    nc.tensor.matmul(m_ps[:, :], ones[:, :], v_abs[:, :], start=True, stop=True
                                     ).then_inc(vrow_sum, 1)

            @block.scalar
            def _(act):
                act.sem_inc(k_copied, 2)
                act.sem_inc(v_copied, 2)
                act.sem_inc(vrow_done, 1)
                act.sem_inc(k_stored, 64)
                act.sem_inc(f_stored, 16)
                for s in range(VB):
                    act.sem_inc(v_stored[s], 16)
                for i in range(SLICES):
                    act.wait_ge(w_landed[i % MT], 16 * (i // MT + 1))
                    nc.scalar.copy(w_hi[:, i, :], v_all[:, i % MT, :]).then_inc(w_hi_done, 1)
                with act.Fori(0, B) as b:
                    with act.Fori(0, MT // 2) as u:
                        for j in range(2):
                            t = b * MT + u * 2 + j
                            act.wait_ge(k_sum, t + 1)
                            act.wait_ge(k_turned, t + 1)
                            nc.scalar.copy(k_nat[:, :], k_ps[j][:, :]).then_inc(k_copied, 1)
                            act.wait_ge(v_sum, t + 3)
                            act.wait_ge(v_lo_done, t + 1)
                            nc.scalar.copy(v_all[:, u * 2 + j, :], v_ps[j][:, :]).then_inc(v_copied, 1)
                            act.wait_ge(k_turned, t + 2)
                            act.wait_ge(k_stored, 64 * t + 64)
                            nc.scalar.copy(k_hi[:, :, :], t_ps.rearrange("p (ct m) -> p ct m", m=P)
                                           ).then_inc(k_hi_done, 1)
                            act.wait_ge(k_lo_done, t + 2)
                            for part, src in enumerate((k_hi, k_lo)):
                                for hh in range(2):
                                    act.dma_start(k_dst[b, part, hh, u * 2 + j],
                                                  src[hh * DK:(hh + 1) * DK, :, :].bitcast(F32)
                                                  ).then_inc(k_stored, 16)
                    act.wait_ge(vrow_sum, b + 2)
                    act.wait_ge(v_scaled, MT * b + MT)
                    nc.scalar.copy(v_row[:, :], m_ps[:, :]).then_inc(vrow_done, 1)
                    act.dma_start(f_scr[b], v_fac[:, :]).then_inc(f_stored, 16)
                    for i in range(MT + 1):
                        if i < MT:
                            act.wait_ge(v_scaled, MT * b + MT + i + 1)
                            act.wait_ge(v_stored[i % VB], 16 * (b * (MT // VB) + i // VB + 1))
                            nc.scalar.copy(v_parts[:, i % VB, :, 0], tiles(v_all[:, i, :])).then_inc(v_hi_done, 1)
                        if i:
                            act.wait_ge(v_lo_done, MT * b + MT + i)
                            act.dma_start(v_scr[b, :, :, i - 1].rearrange("ct m s c -> m ct (s c)"),
                                          v_parts[:, (i - 1) % VB].rearrange("m ct s c -> m ct (s c)")
                                          ).then_inc(v_stored[(i - 1) % VB], 16)
                act.wait_ge(k_stored, 64 * (B * MT + 1))
                act.wait_ge(f_stored, 16 * (B + 1))
                for s in range(VB):
                    act.wait_ge(v_stored[s], 16 * (B * MT // VB + 1))

            def split_v(dve, b, i):
                dve.wait_ge(v_hi_done, MT * b + i + 1)
                nc.vector.tensor_tensor(v_parts[:, i % VB, :, 1], tiles(v_all[:, i, :]), v_parts[:, i % VB, :, 0],
                                        ALU.subtract).then_inc(v_lo_done, 1)

            @block.vector
            def _(dve):
                dve.sem_inc(k_lo_done, 1)
                dve.sem_inc(v_scaled, MT)
                dve.sem_inc(v_lo_done, MT)
                for i in range(SLICES):
                    dve.wait_ge(w_hi_done, i + 1)
                    nc.vector.tensor_tensor(w_lo[:, i, :], v_all[:, i % MT, :], w_hi[:, i, :],
                                            ALU.subtract).then_inc(w_lo_done, 1)

                def split_k(t):
                    dve.wait_ge(k_hi_done, t + 1)
                    nc.vector.tensor_tensor(k_lo[:, :, :], t_ps.rearrange("p (ct m) -> p ct m", m=P),
                                            k_hi[:, :, :], ALU.subtract).then_inc(k_lo_done, 1)

                with dve.Fori(0, B) as b:
                    with dve.Fori(0, MT - 1) as i:
                        split_k(b * MT + i)
                    dve.wait_ge(v_copied, MT * b + MT + 1)
                    dve.wait_ge(vrow_sum, b + 1)
                    nc.vector.tensor_reduce(v_abs[:, :], v_all[:, 0:MT - 1].rearrange("p t c -> p c t"), AX.X,
                                            ALU.max, apply_absolute_value=True).then_inc(abs_steps, 1)
                    split_k(b * MT + MT - 1)
                    dve.wait_ge(v_copied, MT * b + MT + 2)
                    dve.wait_ge(abs_steps, 2 * b + 1)
                    nc.vector.scalar_tensor_tensor(out=v_abs[:, :], in0=v_all[:, MT - 1, :], scalar=-1.0,
                                                   in1=v_abs[:, :], op0=ALU.mult, op1=ALU.max
                                                   ).then_inc(abs_steps, 1)
                    dve.wait_ge(abs_steps, 2 * b + 2)
                    nc.vector.tensor_tensor(v_abs[:, :], v_all[:, MT - 1, :], v_abs[:, :], ALU.max
                                            ).then_inc(abs_done, 1)
                    dve.wait_ge(abs_turned, b + 1)
                    nc.vector.tensor_reduce(v_max[:, :], m_ps.rearrange("p (ct m) -> p ct m", m=P),
                                            AX.X, ALU.max).then_inc(vmax_steps, 1)
                    dve.wait_ge(vmax_steps, 4 * b + 1)
                    nc.vector.tensor_scalar(v_div[:, :], v_max[:, :], TINY, 1.0 / V_SCALE, ALU.max,
                                            ALU.mult).then_inc(vmax_steps, 1)
                    dve.wait_ge(vmax_steps, 4 * b + 2)
                    nc.vector.reciprocal(v_inv[:, :], v_div[:, :]).then_inc(vmax_steps, 1)
                    dve.wait_ge(f_stored, 16 * b + 16)
                    nc.vector.tensor_scalar(v_fac[:, :], v_div[:, :], 1.0 / P_SCALE, None,
                                            ALU.mult).then_inc(vmax_steps, 1)
                    dve.wait_ge(vmax_steps, 4 * b + 4)
                    for ct in range(CT):
                        last = nc.vector.tensor_scalar(v_abs[:, ct * P:(ct + 1) * P], ident[:, :],
                                                       v_inv[:, ct:ct + 1], None, ALU.mult)
                    last.then_inc(vdiag_done, 1)
                    dve.wait_ge(vrow_done, b + 2)
                    for i in range(MT):
                        nc.vector.tensor_tensor(v_all[:, i, :], v_all[:, i, :], v_row[:, :], ALU.mult
                                                ).then_inc(v_scaled, 1)
                        if i:
                            split_v(dve, b, i - 1)
                    split_v(dve, b, MT - 1)


def attention(nc, x_chunks, wq, wp, bias, ident, stats, k_scr, v_scr, f_scr, p_scr,
              B, C, CT, NR, MT, CH, NCH, DK):
    CHUNKS = B * NCH
    PU, NT = 8, CH // P
    CP = CT
    PAIRS, UNITS, TILES = CHUNKS * CP, CHUNKS * CP * PU, CHUNKS * CT
    assert PU == 2 * NT and CT == 4
    SCALE = float(DK) ** -0.5
    assert SCALE == 0.125
    with ExitStack() as ctx:
        def sb(name, shape, dt=F32):
            return ctx.enter_context(nc.sbuf_tensor(name, shape, dt))

        def psum(name, n=1):
            return ctx.enter_context(nc.psum_tensor(name, [P, n * CH], F32))

        def sem(name):
            return ctx.enter_context(nc.semaphore(name))

        k_sb = sb("k_sb", [P, 2, 2, NR], F32R)
        v_sb = sb("v_sb", [P, 2, MT, 2, P], F16)
        f_sb = sb("f_sb", [P, CP, CT])
        wq_hi = sb("wq_hi", [P, CT, C], F32R)
        wq_lo = sb("wq_lo", [P, CT, C], F32R)
        wp_hi = sb("wp_hi", [P, CT, C], F32R)
        wp_lo = sb("wp_lo", [P, CT, C], F32R)
        x_in = sb("x2_in", [P, 2, CH])
        x_hi = sb("x2_hi", [P, CT, CH], F32R)
        x_lo = sb("x2_lo", [P, CT, CH], F32R)
        q_x = sb("q_x", [P, 2, 2, CH], F32R)
        q_y = sb("q_y", [P, 2, 2, CH], F32R)
        probs = sb("probs", [P, 2, NR])
        pt_hi = sb("pt_hi", [P, 2, 2, MT, CH], F16)
        pt_lo = sb("pt_lo", [P, 2, 2, MT, CH], F16)
        neg_max = sb("neg_max", [P, 2])
        shift = sb("shift", [P, 2])
        ones = sb("ones2", [P, P])
        bias_sb = sb("bias_sb", [P, NH])
        sums = sb("sums", [P, 2, NT, 2])
        inv = sb("inv", [P, NT, 2])
        inv_wide = sb("inv_wide", [P, 2, 2, DK])
        spread = sb("spread", [P, CH])
        o_sb = sb("o_sb", [P, CH])
        o_hi = sb("o_hi", [P, 2, CT, CH], F32R)
        o_lo = sb("o_lo", [P, 2, CT, CH], F32R)
        proj = sb("proj", [P, CH])

        s_ps = [psum(f"s_ps{i}", 2) for i in range(2)]
        t_ps = [psum(f"t2_ps{i}") for i in range(2)]
        pv_ps = psum("pv_ps")
        g_ps = psum("g_ps")

        w_landed = [sem(f"w2_landed{i}") for i in range(2 * CT)]
        w_hi_done = sem("w2_hi_done")
        w_lo_done = sem("w2_lo_done")
        bias_landed = sem("bias_landed")
        x0_landed = sem("x2_first_landed")
        x_landed = [sem(f"x2_landed{i}") for i in range(2)]
        x_hi_done = sem("x2_hi_done")
        x_lo_done = sem("x2_lo_done")
        loads = sem("loads")
        k_landed = [sem(f"k_landed{i}") for i in range(2)]
        v_landed = [sem(f"v_landed{i}") for i in range(2)]
        q_sum = sem("q_sum")
        q_hi_done = sem("q_hi_done")
        q_lo_done = sem("q_lo_done")
        q_doubled = [[sem(f"q_doubled{i}{h}") for h in range(2)] for i in range(2)]
        scores_ready = sem("scores_ready")
        max_done = sem("max_done")
        shift_done = sem("shift_done")
        ones_made = sem("ones_made")
        exp_done = sem("exp_done")
        turned = sem("turned")
        pt_hi_done = sem("pt_hi_done")
        pt_lo_done = sem("pt_lo_done")
        pv_sum = sem("pv_sum")
        inv_done = sem("inv_done")
        wide_done = sem("wide_done")
        spread_sum = sem("spread_sum")
        spread_done = sem("spread_done")
        o_done = sem("o_done")
        o_hi_done = sem("o_hi_done")
        o_lo_done = sem("o_lo_done")
        proj_sum = sem("proj_sum")
        proj_done = sem("proj_done")
        stats_done = sem("stats_done")
        proj_stored = sem("proj_stored")

        w_in = (probs.rearrange("p u (h n) -> p (u h) n", h=NR // C),
                pt_lo[:, 1, 0].bitcast(F32).rearrange("p t n -> p (t n)").rearrange("p (ct n) -> p ct n", n=C))
        x0_in = pt_hi[:, 1, 0].bitcast(F32).rearrange("p t n -> p (t n)").rearrange("p (ct n) -> p ct n", n=CH)
        TERMS = ((wq_hi, x_hi), (wq_lo, x_hi), (wq_hi, x_lo))

        def tile_at(c, p):
            return (c - 1, p - 2) if p >= 2 else (c - 2, p + 2)

        def pair_at(c, p, back):
            return (c, p - back) if p >= back else (c - 1, p - back + CP)

        def x_load(sp, c, ct):
            wait(sp, x_lo_done, CT * c + ct - 1)
            sp.dma_start(x_in[:, ct % 2, :], x_chunks[c // NCH, c % NCH, :, ct]).then_inc(x_landed[ct % 2], 16)

        def k_load(sp, c, p):
            wait(sp, scores_ready, PU * (CP * c + p - 1))
            sp.sem_inc(loads, 1)
            for hh in range(2):
                sp.dma_start(k_sb[:, p % 2, hh, :].bitcast(F32),
                             k_scr[c // NCH, 2 * p + hh].rearrange("s d m -> (s d) m")
                             ).then_inc(k_landed[p % 2], 16)

        def v_load(sp, c, p):
            wait(sp, pv_sum, CP * c + p - 1)
            sp.sem_inc(loads, 1)
            sp.dma_start(v_sb[:, p % 2], v_scr[c // NCH, p]).then_inc(v_landed[p % 2], 16)
            sp.dma_start(f_sb[:, p, :], f_scr[c // NCH]).then_inc(v_landed[p % 2], 16)

        def q_double(sp, pair, par):
            for hh in range(2):
                own, other = slice(hh * DK, (hh + 1) * DK), slice((1 - hh) * DK, (2 - hh) * DK)
                sp.wait_ge(q_lo_done, 2 * pair + hh + 1)
                sp.dma_start(q_x[other, par, hh, :].bitcast(F32), q_y[own, par, hh, :].bitcast(F32)
                             ).then_inc(q_doubled[par][hh], 16)
                sp.dma_start(q_y[other, par, hh, :].bitcast(F32), q_x[own, par, hh, :].bitcast(F32)
                             ).then_inc(q_doubled[par][hh], 16)

        with nc.Block() as block:

            @block.sync
            def _(sp):
                sp.dma_start(x0_in, x_chunks[0, 0]).then_inc(x0_landed, 16)
                for i in range(2 * CT):
                    src = (wq, wp)[i // CT][(i % CT) * P:(i % CT + 1) * P, :]
                    sp.dma_start(w_in[i // CT][:, i % CT, :], src).then_inc(w_landed[i], 16)
                    if i == CT - 1:
                        k_load(sp, 0, 0)
                        sp.dma_start(bias_sb[:, :], bias.to_broadcast([P, NH])).then_inc(bias_landed, 16)
                q_double(sp, 0, 0)

                def chunk(c):
                    for p in range(CP):
                        pair = CP * c + p
                        if there(pair + 1, PAIRS):
                            k_load(sp, *((c, p + 1) if p + 1 < CP else (c + 1, 0)))
                        if there(pair, PAIRS):
                            v_load(sp, c, p)
                        if p == 1 and there(c + 1, CHUNKS):
                            x_load(sp, c + 1, 0)
                            x_load(sp, c + 1, 1)
                        cc, mo = tile_at(c, p)
                        if there(cc * CT + mo, TILES):
                            sp.wait_ge(proj_done, cc * CT + mo + 1)
                            sp.dma_start(p_scr[cc, mo], proj[:, :]).then_inc(proj_stored, 16)
                        if there(pair + 1, PAIRS):
                            q_double(sp, pair + 1, (p + 1) % 2)
                        if p == 2 and there(c + 1, CHUNKS):
                            x_load(sp, c + 1, 2)
                            x_load(sp, c + 1, 3)

                for c in range(2):
                    chunk(c)
                with sp.Fori(2, CHUNKS - 1) as c:
                    chunk(c)
                for c in range(CHUNKS - 1, CHUNKS + 2):
                    chunk(c)
                sp.wait_ge(proj_stored, 16 * TILES)

            @block.tensor
            def _(pe):
                def o_proj(cc, mo, half):
                    wait(pe, proj_done, cc * CT + mo)
                    pe.wait_ge(w_lo_done, 2 * CT)
                    for kt in (2 * half, 2 * half + 1):
                        pe.wait_ge(o_lo_done, CP * cc + kt + 1)
                        for n, (w, a) in enumerate(((wp_hi, o_hi), (wp_lo, o_hi), (wp_hi, o_lo))):
                            mm = nc.tensor.matmul(g_ps[:, :], w[:, kt, mo * P:(mo + 1) * P],
                                                  a[:, cc % 2, kt, :],
                                                  start=(kt == 0 and n == 0), stop=(kt == CT - 1 and n == 2))
                    if half:
                        mm.then_inc(proj_sum, 1)

                def q_half(c, p, half):
                    for ct in (2 * half, 2 * half + 1):
                        pe.wait_ge(x_lo_done, CT * c + ct + 1)
                        for n, (w, a) in enumerate(TERMS):
                            mm = nc.tensor.matmul(g_ps[:, :], w[:, ct, p * P:(p + 1) * P], a[:, ct, :],
                                                  start=(ct == 0 and n == 0), stop=(ct == CT - 1 and n == 2))
                    if half:
                        mm.then_inc(q_sum, 1)

                def scores(c, p, k):
                    unit, hh, nt = PU * (CP * c + p) + k, k // NT, k % NT
                    if k == 0:
                        pe.wait_ge(k_landed[p % 2], 32 * (CP // 2 * c + p // 2) + 32)
                    if nt == 0:
                        pe.wait_ge(q_doubled[p % 2][hh], 32 * (CP // 2 * c + p // 2) + 32)
                    wait(pe, exp_done, unit - 1)
                    ps = s_ps[k % 2]
                    for n, q in enumerate((q_x, q_y)):
                        for m in range(NR // CH):
                            mm = nc.tensor.matmul(ps[:, m * CH:(m + 1) * CH],
                                                  q[:, p % 2, hh, nt * P:(nt + 1) * P],
                                                  k_sb[:, p % 2, hh, m * CH:(m + 1) * CH],
                                                  start=(n == 0), stop=(n == 1))
                    mm.then_inc(scores_ready, 1)

                def turn(unit, k):
                    pe.wait_ge(exp_done, unit + 1)
                    for half in range(2):
                        wait(pe, pt_lo_done, 2 * unit - 1 + half)
                        for i in range(MT // 2):
                            m = half * (MT // 2) + i
                            mm = nc.tensor.transpose(t_ps[half][:, i * P:(i + 1) * P],
                                                     probs[:, k % 2, m * P:(m + 1) * P], ident[:, :])
                        mm.then_inc(turned, 1)

                def pv(c, p, part):
                    pair = CP * c + p
                    if part == 0:
                        pe.wait_ge(v_landed[p % 2], 32 * (CP // 2 * c + p // 2) + 32)
                        pe.wait_ge(pt_lo_done, 2 * PU * (pair + 1))
                        wait(pe, o_done, pair)
                    for mt in range(part * MT // 4, (part + 1) * MT // 4):
                        for n, (v, pt) in enumerate(((0, pt_hi), (1, pt_hi), (0, pt_lo))):
                            for hh in range(2):
                                own = slice(hh * DK, (hh + 1) * DK)
                                mm = nc.tensor.matmul(pv_ps[own, :], v_sb[:, p % 2, mt, v, own],
                                                      pt[:, p % 2, hh, mt, :],
                                                      start=(mt == 0 and n == 0), stop=(mt == MT - 1 and n == 2),
                                                      skip_group_check=True)
                    if part == 3:
                        mm.then_inc(pv_sum, 1)

                def spread_inv(pair, half):
                    pe.wait_ge(wide_done, 2 * pair + half + 1)
                    for i in range(2):
                        nt = 2 * half + i
                        mm = nc.tensor.transpose(g_ps[:, nt * P:(nt + 1) * P],
                                                 inv_wide[:, i].rearrange("p h d -> p (h d)"), ident[:, :])
                    mm.then_inc(spread_sum, 1)

                def chunk(c):
                    for p in range(CP):
                        pair = CP * c + p
                        cc, mo = tile_at(c, p)
                        for k in range(PU):
                            unit = PU * pair + k
                            if there(unit, UNITS):
                                scores(c, p, k)
                            if there(unit - 1, UNITS):
                                turn(unit - 1, (k - 1) % PU)
                            if k < 2 and there(cc * CT + mo, TILES):
                                if k == 0 and there(pair - 2, PAIRS):
                                    pe.wait_ge(spread_done, pair - 1)
                                o_proj(cc, mo, k)
                            if k in (2, 3) and there(pair + 1, PAIRS):
                                if k == 2 and there(cc * CT + mo, TILES):
                                    pe.wait_ge(proj_done, cc * CT + mo + 1)
                                elif k == 2 and there(pair - 2, PAIRS):
                                    pe.wait_ge(spread_done, pair - 1)
                                q_half(*((c, p + 1) if p + 1 < CP else (c + 1, 0)), k - 2)
                            if k >= 4 and there(pair - 1, PAIRS):
                                if k == 6:
                                    if there(pair + 1, PAIRS):
                                        pe.wait_ge(q_lo_done, 2 * pair + 4)
                                    elif there(cc * CT + mo, TILES):
                                        pe.wait_ge(proj_done, cc * CT + mo + 1)
                                    spread_inv(pair - 1, 0)
                                pv(*pair_at(c, p, 1), k - 4)
                                if k == 6:
                                    spread_inv(pair - 1, 1)

                pe.wait_ge(w_lo_done, CT // 2)
                q_half(0, 0, 0)
                pe.wait_ge(w_lo_done, CT)
                q_half(0, 0, 1)
                for c in range(2):
                    chunk(c)
                with pe.Fori(2, CHUNKS - 1) as c:
                    chunk(c)
                for c in range(CHUNKS - 1, CHUNKS + 2):
                    chunk(c)

            @block.scalar
            def _(act):
                def q_split(pair, par, hh):
                    if hh == 0:
                        act.wait_ge(q_sum, pair + 1)
                        wait(act, scores_ready, PU * (pair - 1))
                    own = slice(hh * DK, (hh + 1) * DK)
                    nc.scalar.mul(q_x[own, par, hh, :], g_ps[own, :], SCALE).then_inc(q_hi_done, 1)

                def pt_split(c, p, k):
                    pair = CP * c + p
                    unit = PU * pair + k
                    if k == 0:
                        wait(act, pv_sum, pair - 1)
                    for half in range(2):
                        act.wait_ge(turned, 2 * unit + half + 1)
                        nc.scalar.mul(
                            pt_hi[:, p % 2, k // NT, half * (MT // 2):(half + 1) * (MT // 2),
                                  (k % NT) * P:(k % NT + 1) * P],
                            t_ps[half].rearrange("p (t n) -> p t n", n=P), P_SCALE).then_inc(pt_hi_done, 1)

                def exps(c, p, k):
                    pair = CP * c + p
                    unit = PU * pair + k
                    if k == 0:
                        wait(act, inv_done, pair - 1)
                    act.wait_ge(shift_done, unit + 1)
                    wait(act, turned, 2 * unit - 2)
                    nc.scalar.activation(probs[:, k % 2, :], s_ps[k % 2][:, :], ACT.Exp,
                                         bias=shift[:, k % 2:k % 2 + 1],
                                         accum_out=sums[:, p % 2, k % NT, k // NT:k // NT + 1]
                                         ).then_inc(exp_done, 1)

                def chunk(c):
                    for p in range(CP):
                        pair = CP * c + p
                        cc, mo = tile_at(c, p)
                        c2, p2 = pair_at(c, p, 2)
                        for k in range(PU):
                            unit = PU * pair + k
                            if k == 2 and there(cc * CT + mo, TILES):
                                n = cc * CT + mo
                                act.wait_ge(proj_sum, n + 1)
                                wait(act, stats_done, n)
                                wait(act, proj_stored, 16 * n)
                                nc.scalar.copy(proj[:, :], g_ps[:, :]).then_inc(proj_done, 1)
                            if k in (4, 5) and there(pair + 1, PAIRS):
                                q_split(pair + 1, (p + 1) % 2, k - 4)
                            if there(unit - 1, UNITS):
                                pt_split(*((c, p, k - 1) if k else (*pair_at(c, p, 1), PU - 1)))
                            if there(unit, UNITS):
                                exps(c, p, k)
                            if k == 2 and there(pair - 2, PAIRS):
                                act.wait_ge(o_done, pair - 1)
                                if p2 == 0:
                                    wait(act, proj_sum, CT * (c2 - 1))
                                nc.scalar.copy(o_hi[:, c2 % 2, p2, :], o_sb[:, :]).then_inc(o_hi_done, 1)
                            if k == 6 and there(pair - 1, PAIRS):
                                act.wait_ge(spread_sum, 2 * pair)
                                wait(act, o_done, pair - 1)
                                nc.scalar.copy(spread[:, :], g_ps[:, :]).then_inc(spread_done, 1)

                for i in range(2 * CT):
                    if i == 0:
                        act.wait_ge(x0_landed, 16)
                    if i == CT:
                        q_split(0, 0, 0)
                        q_split(0, 0, 1)
                    if i < CT:
                        nc.scalar.copy(x_hi[:, i, :], x0_in[:, i, :]).then_inc(x_hi_done, 1)
                    act.wait_ge(w_landed[i], 16)
                    nc.scalar.copy((wq_hi, wp_hi)[i // CT][:, i % CT, :], w_in[i // CT][:, i % CT, :]
                                   ).then_inc(w_hi_done, 1)
                for c in range(2):
                    chunk(c)
                with act.Fori(2, CHUNKS - 1) as c:
                    chunk(c)
                for c in range(CHUNKS - 1, CHUNKS + 2):
                    chunk(c)

            @block.vector
            def _(dve):
                def q_split(pair, par, hh):
                    own = slice(hh * DK, (hh + 1) * DK)
                    dve.wait_ge(q_hi_done, 2 * pair + hh + 1)
                    nc.vector.scalar_tensor_tensor(out=q_y[own, par, hh, :], in0=g_ps[own, :], scalar=SCALE,
                                                   in1=q_x[own, par, hh, :], op0=ALU.mult,
                                                   op1=ALU.subtract).then_inc(q_lo_done, 1)

                def pt_split(c, p, k):
                    unit = PU * (CP * c + p) + k
                    for half in range(2):
                        dve.wait_ge(pt_hi_done, 2 * unit + half + 1)
                        at = (slice(None), p % 2, k // NT, slice(half * (MT // 2), (half + 1) * (MT // 2)),
                              slice((k % NT) * P, (k % NT + 1) * P))
                        nc.vector.scalar_tensor_tensor(
                            out=pt_lo[at], in0=t_ps[half].rearrange("p (t n) -> p t n", n=P), scalar=P_SCALE,
                            in1=pt_hi[at], op0=ALU.mult, op1=ALU.subtract).then_inc(pt_lo_done, 1)

                def chunk(c):
                    for p in range(CP):
                        pair = CP * c + p
                        cc, mo = tile_at(c, p)
                        c2, p2 = pair_at(c, p, 2)
                        for k in range(PU):
                            unit = PU * pair + k
                            if there(unit, UNITS):
                                h, b = 2 * p + k // NT, slice(k % 2, k % 2 + 1)
                                dve.wait_ge(scores_ready, unit + 1)
                                wait(dve, exp_done, unit - 1)
                                nc.vector.tensor_reduce(neg_max[:, b], s_ps[k % 2][:, :], AX.X, ALU.max,
                                                        negate=True).then_inc(max_done, 1)
                                dve.wait_ge(max_done, unit + 1)
                                nc.vector.tensor_scalar(shift[:, b], neg_max[:, b], bias_sb[:, h:h + 1],
                                                        bias_sb[:, h:h + 1], ALU.subtract, ALU.add
                                                        ).then_inc(shift_done, 1)
                            if k < 2 and there(pair - 2, PAIRS):
                                if k == 0:
                                    dve.wait_ge(pv_sum, pair - 1)
                                    dve.wait_ge(spread_done, pair - 1)
                                    wait(dve, o_lo_done, pair - 2)
                                half = slice(k * (CH // 2), (k + 1) * (CH // 2))
                                o = nc.vector.scalar_tensor_tensor(
                                    out=o_sb[:, half], in0=pv_ps[:, half], scalar=f_sb[:, p2, p2:p2 + 1],
                                    in1=spread[:, half], op0=ALU.mult, op1=ALU.mult)
                                if k == 1:
                                    o.then_inc(o_done, 1)
                            if k == 1 and there(pair - 1, PAIRS):
                                dve.wait_ge(exp_done, PU * pair)
                                wait(dve, wide_done, 2 * (pair - 1))
                                nc.vector.reciprocal(inv[:, :, :], sums[:, (p - 1) % 2, :, :]
                                                     ).then_inc(inv_done, 1)
                            if k in (4, 5) and there(pair + 1, PAIRS):
                                q_split(pair + 1, (p + 1) % 2, k - 4)
                            if there(unit - 1, UNITS):
                                pt_split(*((c, p, k - 1) if k else (*pair_at(c, p, 1), PU - 1)))
                            if k == 3 and there(cc * CT + mo, TILES):
                                dve.wait_ge(proj_done, cc * CT + mo + 1)
                                nc.vector.bn_stats(stats[:, mo, cc, :], proj[:, :]).then_inc(stats_done, 1)

                for i in range(2 * CT):
                    if i == CT:
                        q_split(0, 0, 0)
                        q_split(0, 0, 1)
                    if i < CT:
                        dve.wait_ge(x_hi_done, i + 1)
                        nc.vector.tensor_tensor(x_lo[:, i, :], x0_in[:, i, :], x_hi[:, i, :], ALU.subtract
                                                ).then_inc(x_lo_done, 1)
                    dve.wait_ge(w_hi_done, i + 1)
                    nc.vector.tensor_tensor((wq_lo, wp_lo)[i // CT][:, i % CT, :], w_in[i // CT][:, i % CT, :],
                                            (wq_hi, wp_hi)[i // CT][:, i % CT, :], ALU.subtract
                                            ).then_inc(w_lo_done, 1)
                dve.wait_ge(bias_landed, 16)
                for c in range(2):
                    chunk(c)
                with dve.Fori(2, CHUNKS - 1) as c:
                    chunk(c)
                for c in range(CHUNKS - 1, CHUNKS + 2):
                    chunk(c)

            @block.gpsimd
            def _(pool):
                def x_split(c, ct):
                    pool.wait_ge(x_landed[ct % 2], 16 * (2 * (c - 1) + ct // 2 + 1))
                    if ct == 0:
                        wait(pool, q_sum, CP * c)
                    nc.gpsimd.tensor_tensor(x_hi[:, ct, :].rearrange("p (i n) -> p i n", n=P),
                                            x_in[:, ct % 2, :].rearrange("p (i n) -> p i n", n=P),
                                            ones.rearrange("p (o n) -> p o n", o=1).to_broadcast([P, CH // P, P]),
                                            ALU.mult).then_inc(x_hi_done, 1)
                    pool.wait_ge(x_hi_done, CT * c + ct + 1)
                    nc.gpsimd.tensor_tensor(x_lo[:, ct, :], x_in[:, ct % 2, :], x_hi[:, ct, :], ALU.subtract
                                            ).then_inc(x_lo_done, 1)

                def widen(pair, half):
                    pool.wait_ge(inv_done, pair + 1)
                    wait(pool, spread_sum, 2 * pair + half)
                    for i in range(2):
                        last = nc.gpsimd.tensor_tensor(
                            inv_wide[:, i], inv[:, 2 * half + i, :].unsqueeze(2).to_broadcast([P, 2, DK]),
                            ones.rearrange("p (h d) -> p h d", d=DK), ALU.mult)
                    last.then_inc(wide_done, 1)

                def chunk(c):
                    for p in range(CP):
                        pair = CP * c + p
                        c2, p2 = pair_at(c, p, 2)
                        for k in range(PU):
                            if k == 1 and there(pair - 1, PAIRS):
                                widen(pair - 1, 0)
                            if k == 6 and there(pair - 1, PAIRS):
                                widen(pair - 1, 1)
                            if k == 3 and there(pair - 2, PAIRS):
                                pool.wait_ge(o_hi_done, pair - 1)
                                nc.gpsimd.tensor_tensor(o_lo[:, c2 % 2, p2, :], o_sb[:, :], o_hi[:, c2 % 2, p2, :],
                                                        ALU.subtract).then_inc(o_lo_done, 1)
                            if p == 2 and k in (4, 7) and there(c + 1, CHUNKS):
                                for ct in ((0, 1) if k == 4 else (2, 3)):
                                    x_split(c + 1, ct)

                nc.gpsimd.memset(ones[:, :], 1.0).then_inc(ones_made, 1)
                pool.wait_ge(ones_made, 1)
                for c in range(2):
                    chunk(c)
                with pool.Fori(2, CHUNKS - 1) as c:
                    chunk(c)
                for c in range(CHUNKS - 1, CHUNKS + 2):
                    chunk(c)


def norms(nc, x_chunks, out_chunks, p_scr, stats, bn_gamma, bn_beta, ln_gamma, ln_beta,
          B, C, CT, CH, NCH):
    CHUNKS = B * NCH
    with ExitStack() as ctx:
        def sb(name, shape, dt=F32):
            return ctx.enter_context(nc.sbuf_tensor(name, shape, dt))

        def sem(name):
            return ctx.enter_context(nc.semaphore(name))

        vecs = sb("vecs", [P, 4, CT])
        moments = sb("moments", [P, CT, 2])
        std = sb("std", [P, CT])
        rstd = sb("rstd", [P, CT])
        eps = sb("eps", [P, 1])
        a_bn = sb("a_bn", [P, CT])
        ma = sb("ma", [P, CT])
        b_bn = sb("b_bn", [P, CT])
        mean_w = sb("mean_w", [P, P])
        x_in = sb("x3_in", [P, 4, CT, CH])
        p_in = sb("p3_in", [P, 4, CT, CH])
        bn = sb("bn", [P, 2, CT, CH])
        y = sb("y", [P, 2, CT, CH])
        d = sb("d", [P, 4, CT, CH])
        sq = sb("sq", [P, 2, CT, CH])
        dev = sb("dev", [P, 2, CH])
        ln = sb("ln", [P, 2, CH])
        z = sb("z", [P, 2, CT, CH])
        o = sb("o", [P, 2, CT, CH])
        mean_ps = [ctx.enter_context(nc.psum_tensor(f"mean_ps{i}", [P, CH], F32)) for i in range(2)]
        var_ps = [ctx.enter_context(nc.psum_tensor(f"var_ps{i}", [P, CH], F32)) for i in range(2)]

        vecs_landed = sem("vecs_landed")
        w_done = sem("mean_w_done")
        coef = sem("coef")
        std_done = sem("std_done")
        x_landed = [sem(f"x3_landed{i}") for i in range(4)]
        p_landed = [sem(f"p3_landed{i}") for i in range(4)]
        bn_done = sem("bn_done")
        y_done = sem("y_done")
        mean_done = sem("mean_done")
        d_done = sem("d_done")
        sq_done = sem("sq_done")
        var_done = sem("var_done")
        dev_done = sem("dev_done")
        ln_done = sem("ln_done")
        z_done = sem("z_done")
        o_done = sem("o3_done")
        stored = [sem(f"stored{i}") for i in range(2)]
        COEFS = CT + 4

        assert CHUNKS % 4 == 0 and CHUNKS >= 12

        def run(eng, step, extra):
            for s in range(8):
                step(s, s % 4, s // 4)
            with eng.Fori(2, CHUNKS // 4 - 1) as u:
                for j in range(4):
                    step(u * 4 + j, j, u)
            for s in range(CHUNKS - 4, CHUNKS + extra):
                step(s, s % 4, s // 4)

        with nc.Block() as block:

            @block.sync
            def _(sp):
                for i, v in enumerate((bn_gamma, bn_beta, ln_gamma, ln_beta)):
                    sp.dma_start(vecs[:, i, :], v).then_inc(vecs_landed, 16)

                def load(s, j):
                    wait(sp, bn_done, s - 3)
                    sp.dma_start(p_in[:, j], p_scr[s].rearrange("ct p n -> p ct n")).then_inc(p_landed[j], 16)
                    wait(sp, y_done, s - 3)
                    sp.dma_start(x_in[:, j], x_chunks[s // NCH, s % NCH]).then_inc(x_landed[j], 16)

                def step(s, j, u):
                    if there(s + 2, CHUNKS):
                        load(s + 2, (j + 2) % 4)
                    if there(s - 4, CHUNKS):
                        sp.wait_ge(o_done, s - 3)
                        sp.dma_start(out_chunks[(s - 4) // NCH, (s - 4) % NCH], o[:, j % 2]
                                     ).then_inc(stored[j % 2], 16)
                load(0, 0)
                load(1, 1)
                run(sp, step, 4)
                for j in range(2):
                    sp.wait_ge(stored[j], 16 * CHUNKS // 2)

            @block.scalar
            def _(act):
                act.wait_ge(w_done, 2)
                act.wait_ge(coef, CT)
                nc.scalar.activation(std[:, :], moments[:, :, 1], ACT.Sqrt, bias=eps[:, :]).then_inc(std_done, 1)
                act.wait_ge(coef, COEFS)
                act.wait_ge(vecs_landed, 64)

                def step(s, j, u):
                    if there(s, CHUNKS):
                        act.wait_ge(p_landed[j], 16 * u + 16)
                        wait(act, y_done, s - 1)
                        for ct in range(CT):
                            last = nc.scalar.activation(bn[:, j % 2, ct], p_in[:, j, ct], ACT.Identity,
                                                        bias=b_bn[:, ct:ct + 1], scale=a_bn[:, ct:ct + 1])
                        last.then_inc(bn_done, 1)
                    if there(s - 3, CHUNKS):
                        act.wait_ge(var_done, s - 2)
                        wait(act, ln_done, s - 4)
                        nc.scalar.activation(dev[:, (j + 1) % 2], var_ps[(j + 1) % 2][:, :], ACT.Sqrt,
                                             bias=eps[:, :]).then_inc(dev_done, 1)
                    if there(s - 2, CHUNKS):
                        act.wait_ge(d_done, s - 1)
                        wait(act, var_done, s - 3)
                        nc.scalar.activation(sq[:, j % 2], d[:, (j + 2) % 4], ACT.Square).then_inc(sq_done, 1)
                    if there(s - 4, CHUNKS):
                        act.wait_ge(z_done, s - 3)
                        wait(act, stored[j % 2], 16 * (2 * u + j // 2 - 2))
                        for ct in range(CT):
                            last = nc.scalar.activation(o[:, j % 2, ct], z[:, j % 2, ct], ACT.Identity,
                                                        bias=vecs[:, 3, ct:ct + 1], scale=vecs[:, 2, ct:ct + 1])
                        last.then_inc(o_done, 1)
                run(act, step, 4)

            @block.gpsimd
            def _(pool):
                nc.gpsimd.memset(mean_w[:, :], 1.0 / C).then_inc(w_done, 1)
                nc.gpsimd.memset(eps[:, :], EPS).then_inc(w_done, 1)

                def step(s, j, u):
                    pool.wait_ge(bn_done, s + 1)
                    pool.wait_ge(x_landed[j], 16 * u + 16)
                    wait(pool, d_done, s - 1)
                    wait(pool, mean_done, s - 1)
                    nc.gpsimd.tensor_tensor(y[:, j % 2], x_in[:, j], bn[:, j % 2], ALU.add).then_inc(y_done, 1)
                run(pool, step, 0)

            @block.tensor
            def _(pe):
                pe.wait_ge(w_done, 2)

                def step(s, j, u):
                    i = (j + 1) % 2
                    if there(s - 1, CHUNKS):
                        pe.wait_ge(y_done, s)
                        wait(pe, d_done, s - 2)
                        for ct in range(CT):
                            mm = nc.tensor.matmul(mean_ps[i][:, :], mean_w[:, :], y[:, i, ct],
                                                  start=(ct == 0), stop=(ct == CT - 1))
                        mm.then_inc(mean_done, 1)
                    if there(s - 2, CHUNKS):
                        pe.wait_ge(sq_done, s - 1)
                        wait(pe, dev_done, s - 3)
                        for ct in range(CT):
                            mm = nc.tensor.matmul(var_ps[j % 2][:, :], mean_w[:, :], sq[:, j % 2, ct],
                                                  start=(ct == 0), stop=(ct == CT - 1))
                        mm.then_inc(var_done, 1)
                run(pe, step, 2)

            @block.vector
            def _(dve):
                for ct in range(CT):
                    nc.vector.bn_aggr(moments[:, ct, :], stats[:, ct].rearrange("p c s -> p (c s)")
                                      ).then_inc(coef, 1)
                dve.wait_ge(coef, CT)
                dve.wait_ge(vecs_landed, 64)
                dve.wait_ge(std_done, 1)
                nc.vector.reciprocal(rstd[:, :], std[:, :]).then_inc(coef, 1)
                dve.wait_ge(coef, CT + 1)
                nc.vector.tensor_tensor(a_bn[:, :], rstd[:, :], vecs[:, 0], ALU.mult).then_inc(coef, 1)
                dve.wait_ge(coef, CT + 2)
                nc.vector.tensor_tensor(ma[:, :], moments[:, :, 0], a_bn[:, :], ALU.mult).then_inc(coef, 1)
                dve.wait_ge(coef, CT + 3)
                nc.vector.tensor_tensor(b_bn[:, :], vecs[:, 1], ma[:, :], ALU.subtract).then_inc(coef, 1)

                def step(s, j, u):
                    i = (j + 1) % 2
                    if there(s - 3, CHUNKS):
                        dve.wait_ge(dev_done, s - 2)
                        wait(dve, z_done, s - 4)
                        nc.vector.reciprocal(ln[:, i, :], dev[:, i, :]).then_inc(ln_done, 1)
                        dve.wait_ge(ln_done, s - 2)
                        wait(dve, o_done, s - 4)
                        nc.vector.tensor_tensor(z[:, i], d[:, (j + 1) % 4],
                                                ln[:, i, :].unsqueeze(1).to_broadcast([P, CT, CH]),
                                                ALU.mult).then_inc(z_done, 1)
                    if there(s - 1, CHUNKS):
                        dve.wait_ge(mean_done, s)
                        wait(dve, sq_done, s - 4)
                        wait(dve, z_done, s - 4)
                        nc.vector.tensor_tensor(d[:, (j + 3) % 4], y[:, i],
                                                mean_ps[i][:, :].unsqueeze(1).to_broadcast([P, CT, CH]),
                                                ALU.subtract).then_inc(d_done, 1)
                run(dve, step, 3)


def kernel(x, L0_conv_Wq, L0_conv_Wk, L0_conv_Wv, L0_conv_bias, L0_conv_Wproj, L0_conv_bn_gamma,
           L0_conv_bn_beta, L0_conv_ln_gamma, L0_conv_ln_beta):
    import numpy as np
    import concourse.bacc as bacc
    from concourse.bass_utils import run_bass_kernel_spmd

    def pointwise(w):
        return np.ascontiguousarray(np.asarray(w)[:, :, 0, 0].T)

    def taps(w):
        w = np.asarray(w)
        return np.ascontiguousarray(w.transpose(1, 2, 3, 0).reshape(w.shape[1], -1, w.shape[0]))

    def column(v):
        return np.ascontiguousarray(np.asarray(v).reshape(-1, P).T)

    arrays = {
        "x": np.ascontiguousarray(x),
        "wq": pointwise(L0_conv_Wq),
        "wk": taps(L0_conv_Wk),
        "wv": taps(L0_conv_Wv),
        "bias": np.ascontiguousarray(np.asarray(L0_conv_bias).reshape(1, -1)),
        "wp": pointwise(L0_conv_Wproj),
        "bn_gamma": column(L0_conv_bn_gamma),
        "bn_beta": column(L0_conv_bn_beta),
        "ln_gamma": column(L0_conv_ln_gamma),
        "ln_beta": column(L0_conv_ln_beta),
    }
    nc = bacc.Bacc("TRN2", target_bir_lowering=False, num_devices=1)
    args = [nc.dram_tensor(n, a.shape, mybir.dt.from_np(a.dtype), kind="ExternalInput").ap()
            for n, a in arrays.items()]
    out = nc.dram_tensor("out", arrays["x"].shape, F32, kind="ExternalOutput").ap()
    conv_attention(nc, *args, out)
    return run_bass_kernel_spmd(nc, [arrays], core_ids=[0]).results[0]["out"]
```
